# Optimizing a Trainium2 kernel written in Bass

```python
import numpy as np
import jax
import jax.numpy as jnp

def _softmax(x, axis=-1):
    return jax.nn.softmax(x, axis=axis)

def _gelu(x):
    return jax.nn.gelu(x, approximate=True)

def _silu(x):
    return jax.nn.silu(x)

def _sigmoid(x):
    return jax.nn.sigmoid(x)

def _layernorm(x, axis=-1, eps=1e-05):
    m = jnp.mean(x, axis=axis, keepdims=True)
    v = jnp.var(x, axis=axis, keepdims=True)
    return (x - m) / jnp.sqrt(v + eps)

def _scatter_add(tgt, idx, src, axis=0):
    return tgt.at[idx].add(src)

def _segment_sum(src, seg, n):
    return jax.ops.segment_sum(src, seg, n)
kernel_name = 'mk_adaln_d1_jaxref_r8_32950c'

def setup_inputs(seed: int=0):
    np.random.seed(seed)
    _w = jnp.asarray

    def _L0_attn_setup():
        import jax, jax.numpy as jnp
        import numpy as np
        D_MODEL = 128
        N_HEADS = 16
        HEAD_D = D_MODEL // N_HEADS
        B, T = (4, 512)
        ROPE_BASE = 10000.0

        def _rope(x):
            Bx, Tx, Dx = x.shape
            half = Dx // 2
            inv_freq = 1.0 / ROPE_BASE ** (jnp.arange(half, dtype=jnp.float32) / half)
            ang = jnp.arange(Tx, dtype=jnp.float32)[:, None] * inv_freq[None, :]
            cos, sin = (jnp.cos(ang), jnp.sin(ang))
            x1 = x[..., 0::2]
            x2 = x[..., 1::2]
            r1 = x1 * cos - x2 * sin
            r2 = x1 * sin + x2 * cos
            out = jnp.stack([r1, r2], axis=-1).reshape(Bx, Tx, Dx)
            return out
        key = jax.random.key(seed)
        k_x, k_q, k_k, k_v = jax.random.split(key, 4)
        x = jax.random.normal(k_x, (B, T, D_MODEL), dtype=jnp.float32)
        bound = np.sqrt(6.0 / (HEAD_D * N_HEADS))
        shp = (HEAD_D, HEAD_D, N_HEADS)
        w_q = jax.random.uniform(k_q, shp, jnp.float32, -bound, bound)
        w_k = jax.random.uniform(k_k, shp, jnp.float32, -bound, bound)
        w_v = jax.random.uniform(k_v, shp, jnp.float32, -bound, bound)
        return {'x': x, 'w_q': w_q, 'w_k': w_k, 'w_v': w_v}
    _L0_attn_in = _L0_attn_setup()

    def _L0_ffn_setup():
        import jax, jax.numpy as jnp
        import numpy as np
        H = 128
        I = 256
        E = 32
        B, S = (4, 256)

        def _grouped_mm(a, w, group_sizes):
            return jax.lax.ragged_dot(a, w, group_sizes)

        def _swiglu(x, gw, uw, dw):
            return jax.nn.silu(x @ gw) * (x @ uw) @ dw
        key = jax.random.key(seed)
        ks = jax.random.split(key, 8)
        scale = 0.02
        inp = {'hidden_states': jax.random.normal(ks[0], (B, S, H), dtype=jnp.float32), 'gate_w': jax.random.normal(ks[1], (H, E), dtype=jnp.float32) * scale, 'shared_gate_w': jax.random.normal(ks[2], (H, I), dtype=jnp.float32) * scale, 'shared_up_w': jax.random.normal(ks[3], (H, I), dtype=jnp.float32) * scale, 'shared_down_w': jax.random.normal(ks[4], (I, H), dtype=jnp.float32) * scale, 'routed_gate_w': jax.random.normal(ks[5], (E, H, I), dtype=jnp.float32) * scale, 'routed_up_w': jax.random.normal(ks[6], (E, H, I), dtype=jnp.float32) * scale, 'routed_down_w': jax.random.normal(ks[7], (E, I, H), dtype=jnp.float32) * scale}
        return inp
    _L0_ffn_in = _L0_ffn_setup()
    _L0_c = _w((lambda *s: np.random.randn(*s).astype(np.float32) * 0.05)(8, 128))
    _L0_wmod = _w((lambda *s: np.random.randn(*s).astype(np.float32) * 0.05)(128, 6 * 128) * 128 ** (-0.5))
    _d = {'L0_attn_x': _L0_attn_in['x'], 'L0_attn_w_q': _L0_attn_in['w_q'], 'L0_attn_w_k': _L0_attn_in['w_k'], 'L0_attn_w_v': _L0_attn_in['w_v'], 'L0_ffn_gate_w': _L0_ffn_in['gate_w'], 'L0_ffn_shared_gate_w': _L0_ffn_in['shared_gate_w'], 'L0_ffn_shared_up_w': _L0_ffn_in['shared_up_w'], 'L0_ffn_shared_down_w': _L0_ffn_in['shared_down_w'], 'L0_ffn_routed_gate_w': _L0_ffn_in['routed_gate_w'], 'L0_ffn_routed_up_w': _L0_ffn_in['routed_up_w'], 'L0_ffn_routed_down_w': _L0_ffn_in['routed_down_w'], 'L0_c': _L0_c, 'L0_wmod': _L0_wmod}
    _x0 = _d['L0_attn_x']
    _d['L0_attn_x'] = jax.random.normal(jax.random.fold_in(jax.random.key(seed), 1), (8, 512, 128), dtype=_x0.dtype)
    del _x0
    return _d

def reference(L0_attn_x, L0_attn_w_q, L0_attn_w_k, L0_attn_w_v, L0_ffn_gate_w, L0_ffn_shared_gate_w, L0_ffn_shared_up_w, L0_ffn_shared_down_w, L0_ffn_routed_gate_w, L0_ffn_routed_up_w, L0_ffn_routed_down_w, L0_c, L0_wmod):

    def _L0_attn_ref(x, w_q, w_k, w_v):
        import jax, jax.numpy as jnp
        import numpy as np
        D_MODEL = 128
        N_HEADS = 16
        HEAD_D = D_MODEL // N_HEADS
        B, T = (4, 512)
        ROPE_BASE = 10000.0

        def _rope(x):
            Bx, Tx, Dx = x.shape
            half = Dx // 2
            inv_freq = 1.0 / ROPE_BASE ** (jnp.arange(half, dtype=jnp.float32) / half)
            ang = jnp.arange(Tx, dtype=jnp.float32)[:, None] * inv_freq[None, :]
            cos, sin = (jnp.cos(ang), jnp.sin(ang))
            x1 = x[..., 0::2]
            x2 = x[..., 1::2]
            r1 = x1 * cos - x2 * sin
            r2 = x1 * sin + x2 * cos
            out = jnp.stack([r1, r2], axis=-1).reshape(Bx, Tx, Dx)
            return out
        Bx, Tx, Dx = x.shape
        d = Dx // N_HEADS
        xh = x.reshape(Bx, Tx, d, N_HEADS)
        q = jnp.einsum('btqh,qdh->btdh', xh, w_q).reshape(Bx, Tx, Dx)
        k = jnp.einsum('btkh,kdh->btdh', xh, w_k).reshape(Bx, Tx, Dx)
        v = jnp.einsum('btvh,vdh->btdh', xh, w_v).reshape(Bx, Tx, Dx)
        q = _rope(q)
        k = _rope(k)
        gamma = 1.0 / jnp.sqrt(jnp.float32(Dx))
        scores = jnp.einsum('bqd,bkd->bqk', q, k) * gamma
        causal = jnp.tril(jnp.ones((Tx, Tx), dtype=bool))
        scores = jnp.where(causal[None], scores, -jnp.inf)
        attn = jax.nn.softmax(scores, axis=-1)
        y = jnp.einsum('bqt,btd->bqd', attn, v)
        return y

    def _L0_ffn_ref(hidden_states, gate_w, shared_gate_w, shared_up_w, shared_down_w, routed_gate_w, routed_up_w, routed_down_w):
        import jax, jax.numpy as jnp
        import numpy as np
        H = 128
        I = 256
        E = 32
        B, S = (4, 256)

        def _grouped_mm(a, w, group_sizes):
            return jax.lax.ragged_dot(a, w, group_sizes)

        def _swiglu(x, gw, uw, dw):
            return jax.nn.silu(x @ gw) * (x @ uw) @ dw
        b, s, h = hidden_states.shape
        x = hidden_states.reshape(-1, h)
        shared_out = _swiglu(x, shared_gate_w, shared_up_w, shared_down_w)
        logits = x @ gate_w
        topk_ids = jnp.argmax(logits, axis=-1)
        topk_val = jnp.max(logits, axis=-1)
        scores = jax.nn.sigmoid(topk_val)[:, None]
        xs = x * scores
        tokens_per_expert = jnp.zeros((E,), jnp.int32).at[topk_ids].add(1)
        order = jnp.argsort(topk_ids)
        sorted_x = xs[order]
        g = _grouped_mm(sorted_x, routed_gate_w, tokens_per_expert)
        u = _grouped_mm(sorted_x, routed_up_w, tokens_per_expert)
        d = _grouped_mm(jax.nn.silu(g) * u, routed_down_w, tokens_per_expert)
        inv = jnp.argsort(order)
        routed_out = d[inv]
        return (shared_out + routed_out).reshape(b, s, h)
    x = L0_attn_x
    mod = (_silu(L0_c) @ L0_wmod).reshape(L0_c.shape[0], 6, 1, -1)
    sa, ca, ga, sb, cb, gb = (mod[:, 0], mod[:, 1], mod[:, 2], mod[:, 3], mod[:, 4], mod[:, 5])
    ga = (2 * (ga >= 0) - 1) * jnp.maximum(jnp.abs(ga), 0.25)
    gb = (2 * (gb >= 0) - 1) * jnp.maximum(jnp.abs(gb), 0.25)
    h = _layernorm(x, axis=-1) * (1 + ca) + sa
    x = x + ga * _L0_attn_ref(h, L0_attn_w_q, L0_attn_w_k, L0_attn_w_v)
    h = _layernorm(x, axis=-1) * (1 + cb) + sb
    x = x + gb * _L0_ffn_ref(h, L0_ffn_gate_w, L0_ffn_shared_gate_w, L0_ffn_shared_up_w, L0_ffn_shared_down_w, L0_ffn_routed_gate_w, L0_ffn_routed_up_w, L0_ffn_routed_down_w)
    return x

_drawn_inputs = setup_inputs


def setup_inputs(seed=0):
    import zlib

    import numpy as np

    out = dict(_drawn_inputs(seed))
    spreads = {}
    factors = {'L0_attn_w_q': 8.0,
     'L0_attn_w_k': 8.0,
     'L0_attn_w_v': 5.887,
     'L0_ffn_gate_w': 8.0,
     'L0_ffn_shared_gate_w': 8.0,
     'L0_ffn_shared_up_w': 8.0,
     'L0_ffn_shared_down_w': 8.0,
     'L0_ffn_routed_gate_w': 8.0,
     'L0_ffn_routed_up_w': 8.0,
     'L0_ffn_routed_down_w': 8.0,
     'L0_c': 5.719,
     'L0_wmod': 5.601}
    for name, (base, spread) in spreads.items():
        noise = np.random.default_rng([zlib.crc32(name.encode()), seed]).standard_normal(out[name].shape)
        drawn = base * np.exp(spread * noise) if base else spread * noise
        out[name] = jnp.asarray(drawn.astype(out[name].dtype))
    for name, factor in factors.items():
        out[name] = (out[name] * factor).astype(out[name].dtype)
    return out
```

```python
from contextlib import ExitStack

import concourse.bass as bass
from concourse import mybir

F32 = mybir.dt.float32
BF16 = mybir.dt.bfloat16
I32 = mybir.dt.int32
ALU = mybir.AluOpType
ACT = mybir.ActivationFunctionType
AX = mybir.AxisListType

P = 128
D = 128
NB = 8
T = 512
TILES = T // P
HEADS = 16
HEAD_D = D // HEADS
E = 32
F = 256
FC = F // P
TOKENS = NB * T
BLOCKS = (TOKENS - E) // P + E
BLOCKS_PER_LOAD = 8
ROW = D + 1
GAMMA = float(D) ** -0.5
EPS = 1e-5
FLOOR = 0.25

C_ID, C_UP, C_MASK, C_HEAD = 0, P, 2 * P, 3 * P
C_COS = 4 * P
C_SIN = C_COS + TILES * D
C_REV = C_SIN + TILES * D // 2
C_ROW = C_REV + E
C_ALL = C_ROW + 1


class At:

    def __init__(self, k, i=None, period=2):
        self.k, self.i, self.period = k, i, period

    def __add__(self, n):
        return At(self.k + n, self.i, self.period)

    def count(self, per, extra):
        c = per * self.k + extra
        return c if self.i is None else self.i * (per * self.period) + c

    @property
    def number(self):
        return self.count(1, 0)

    def turn(self, ring, per=1, extra=0):
        c = per * (self.k // ring) + extra
        return c if self.i is None else self.i * (per * self.period // ring) + c


def transposes_in_order():
    order = [("n1", 0)]
    for b in range(NB + 1):
        now, nxt, prev = b < NB, b + 1 < NB, b > 0
        order += [("qk0", b), ("qk1", b)] * now + [("n1", b + 1)] * nxt
        order += [("p0", b), ("p1", b)] * now + [("n2", b - 1)] * prev
        order += [("p2", b), ("p3", b)] * now + [("h2", b - 1)] * prev
    return {use: n for n, use in enumerate(order)}


USES = transposes_in_order()
USES_PER_BATCH = 9
USES_OF_BANK = [(len(USES) + 1) // 2, len(USES) // 2]
SORT_STEPS = 3 + (E.bit_length() - 1) + 2


def use_of(kind, b):
    n = USES[kind, b.k]
    bank, before = n % 2, n // 2
    return bank, before if b.i is None else b.i * USES_PER_BATCH + before


def block_program(nc, x, w_q, w_k, w_v, gate_w, sg_w, su_w, sd_w, rg_w, ru_w, rd_w, c, wmod, table, sel, out):
    with ExitStack() as ctx:
        def sb(name, shape, dt=F32):
            return ctx.enter_context(nc.sbuf_tensor(name, shape, dt))

        def sem(name):
            return ctx.enter_context(nc.semaphore(name))

        bank = [ctx.enter_context(nc.psum_tensor(f"bank{n}", [P, 512], F32)) for n in range(8)]
        sorted_rows = nc.dram_tensor("sorted_rows", (BLOCKS * P, ROW), F32).ap()
        routed_rows = nc.dram_tensor("routed_rows", (TOKENS, D), F32).ap()

        w_gu = sb("w_gu", [P, E, 2 * F])
        x_all = sb("x_all", [P, NB, TILES, D])
        h2t_all = sb("h2t_all", [P, NB, T])
        xs_all = sb("xs_all", [P, NB, TILES, D])
        tab = sb("tab", [P, C_ALL])
        w_v_full = sb("w_v_full", [P, D])
        w_qkv = sb("w_qkv", [P, 2, 3 * D])
        w_router = sb("w_router", [P, E])
        w_sgu = sb("w_sgu", [P, 2, F])
        w_sd = sb("w_sd", [P, FC, D])
        gate_rows = sb("gate_rows", [P, NB, 2, D])
        mod_cols = sb("mod_cols", [P, 4, NB])
        ident_b = sb("ident_b", [P, P], BF16)
        upper_b = sb("upper_b", [P, P], BF16)
        mask_b = sb("mask_b", [P, P], BF16)
        ones_b = sb("ones_b", [P, P], BF16)
        onehot = sb("onehot", [P, NB, TILES + 1, E], BF16)
        rank_all = sb("rank_all", [P, NB, TILES])
        ids_all = sb("ids_all", [P, NB, TILES], I32)
        pos_all = sb("pos_all", [P, NB, TILES], I32)
        blank = sb("blank", [P, ROW])
        minus_half = sb("minus_half", [P, TILES])

        arena = sb("arena", [P, 10 * 1024])

        def carver(part):
            at = [0]

            def carve(*shape):
                n = 1
                for size in shape:
                    n *= size
                piece = part[:, at[0]:at[0] + n]
                at[0] += n
                names = "abc"[:len(shape)]
                return piece.rearrange(f"p ({' '.join(names)}) -> p {' '.join(names)}", **dict(zip(names, shape)))

            return carve

        carve = carver(arena)
        normed = carve(2, TILES, D)
        ht = carve(2, T)
        qkv = carve(2, TILES, 3 * D)
        rot = carve(TILES, 2 * D)
        qkt = carve(2, T)
        probs = carve(2, T)
        probs_t = carve(2, TILES, P)
        rope_c = carve(2, 2 * D)
        rope_s = carve(2, 2 * D)
        w_down = arena[:, 0:E * FC * D].rearrange("p (e c n) -> p e c n", e=E, c=FC)
        w_gu_flat = w_gu[:, :, :].rearrange("p e n -> p (e n)")
        w_down_flat = arena[:, 0:E * FC * D]
        base_wide = arena[:, E * FC * D:E * FC * D + NB * TILES * E].rearrange("p (b j e) -> p b j e", b=NB, j=TILES)
        sh_act_t = arena[:, E * FC * D:E * FC * D + 2 * FC * T].rearrange("p (r c t) -> p r c t", r=2, c=FC)

        normed2 = sb("normed2", [P, TILES, D])
        ht2 = sb("ht2", [P, 2, T])

        stats = sb("stats", [P, 2, TILES, 6])
        mean_var = sb("mean_var", [P, 2, TILES, 2])
        var_eps = sb("var_eps", [P, 2, TILES])
        rstd = sb("rstd", [P, 2, TILES])
        neg_max = sb("neg_max", [P, TILES])
        row_sum = sb("row_sum", [P, 2, TILES])
        row_inv = sb("row_inv", [P, TILES])
        top_logit = sb("top_logit", [P, 2, TILES])
        tied = sb("tied", [P, TILES, E])
        first = sb("first", [P, TILES])
        top_exp = sb("top_exp", [P, 2, TILES])
        top_den = sb("top_den", [P, TILES])
        score = sb("score", [P, 2, TILES])
        ranks = sb("ranks", [P, 2, TILES + 1, E])
        own_rank = sb("own_rank", [P, TILES, E])
        c_cols = sb("c_cols", [P, NB])
        c_exp = sb("c_exp", [P, NB])
        c_den = sb("c_den", [P, NB])
        c_inv = sb("c_inv", [P, NB])
        c_silu = sb("c_silu", [P, NB])
        g_sign = sb("g_sign", [NB, 2 * D])
        g_abs = sb("g_abs", [NB, 2 * D])
        g_rows = sb("g_rows", [NB, 2 * D])
        n_pad = sb("n_pad", [P, E], I32)
        n_blocks = sb("n_blocks", [P, E], I32)
        PAD = E // 2
        ends = sb("ends", [P, 2, PAD + E])
        base = sb("base", [P, E])
        base_own = sb("base_own", [P, NB * TILES])
        before_me = sb("before_me", [P, E])
        expert_col = sb("expert_col", [P, 1])
        expert_row = sb("expert_row", [1, P], I32)

        xs_ring = sb("xs_ring", [P, 2, TILES, ROW])
        pos_ring = sb("pos_ring", [P, 2, TILES], I32)
        sh_silu = sb("sh_silu", [P, FC, T])
        sh_gated = sb("sh_gated", [P, TILES, D])
        carve = carver(xs_all[:, :, :, :].rearrange("p b j d -> p (b j d)"))
        rows_in = carve(4, ROW)
        rows_t = carve(2, P)
        r_silu = carve(2, F)
        r_act = carve(2, F)
        r_act_t = carve(2, FC, P)
        rows_out = carve(4, D)
        ids_out = sb("ids_out", [P, 4], I32)
        carve = carver(xs_all[:, :, :, :].rearrange("p b j d -> p (b j d)"))
        sel_all = carve(NB, P)
        sel_sb = sel_all[0:NB]
        wmod_sb = carve(6 * D)
        w_rep = carve(3, D)
        base_tiles = h2t_all

        ident = tab[:, C_ID:C_ID + P]
        cosines = tab[:, C_COS:C_SIN].rearrange("p (j d) -> p j d", j=TILES)
        sines = tab[:, C_SIN:C_REV].rearrange("p (j d) -> p j d", j=TILES)
        reversed_e = tab[:, C_REV:C_REV + E]
        row_number = tab[:, C_ROW:C_ROW + 1]
        x_tok = x.rearrange("b (j p) d -> p b j d", p=P)
        out_tok = out.rearrange("b (j p) d -> p b j d", p=P)
        routed_tok = routed_rows.rearrange("(b j p) d -> p b j d", p=P, j=TILES)

        s_table = sem("s_table")
        s_cond = sem("s_cond")
        s_weights = sem("s_weights")
        s_x = [sem("s_x_first"), sem("s_x_rest")]
        s_shared_w = sem("s_shared_w")
        s_routed_w = sem("s_routed_w")
        s_down_w = sem("s_down_w")
        blank_made = sem("blank_made")
        blank_kept = sem("blank_kept")
        ids_made = sem("ids_made")
        consts_made = sem("consts_made")
        CONSTS = 6
        pool_consts = sem("pool_consts")
        c_exp_done = sem("c_exp_done")
        c_step = sem("c_step")
        mod_full = sem("mod_full")
        mod_out = sem("mod_out")
        g_step = sem("g_step")
        G_STEPS = 5
        rows_full = sem("rows_full")
        rows_out_done = sem("rows_out_done")
        w_made = sem("w_made")
        wv_ready = sem("wv_ready")
        stat_done = sem("stat_done")
        aggr_done = sem("aggr_done")
        eps_done = sem("eps_done")
        rstd_done = sem("rstd_done")
        norm1_done = sem("norm1_done")
        norm2_done = sem("norm2_done")
        t_full = [sem("t_full0"), sem("t_full1")]
        t_out = [sem("t_out0"), sem("t_out1")]
        q_full = [sem("q_full0"), sem("q_full1")]
        q_out = [sem("q_out0"), sem("q_out1")]
        cos_done = sem("cos_done")
        sin_done = sem("sin_done")
        rot_done = sem("rot_done")
        s_full = sem("s_full")
        max_done = sem("max_done")
        exp_done = sem("exp_done")
        y_full = sem("y_full")
        inv_done = sem("inv_done")
        x2_done = sem("x2_done")
        h2t_kept = [sem("h2t_kept0"), sem("h2t_kept1")]
        r_full = sem("r_full")
        r_step = sem("r_step")
        top_done = sem("top_done")
        sig_exp = sem("sig_exp")
        score_done = sem("score_done")
        onehot_done = sem("onehot_done")
        rank_step = sem("rank_step")
        rank_done = sem("rank_done")
        sort_step = sem("sort_step")
        pos_done = sem("pos_done")
        expert_full = sem("expert_full")
        expert_done = sem("expert_done")
        gu_full = sem("gu_full")
        silu_done = sem("silu_done")
        act_done = sem("act_done")
        d_full = sem("d_full")
        gated = sem("gated")
        base_done = sem("base_done")
        xs_in = [sem("xs_in0"), sem("xs_in1")]
        ids_in = sem("ids_in")
        scattered = [sem("scattered0"), sem("scattered1")]
        rows_in_s = [sem(f"rows_in_s{n}") for n in range(4)]
        ids_kept = sem("ids_kept")
        c_tfull = sem("c_tfull")
        c_tout = sem("c_tout")
        c_gfull = sem("c_gfull")
        c_silu_done = sem("c_silu_done")
        c_act = sem("c_act")
        c_afull = sem("c_afull")
        c_aout = sem("c_aout")
        c_dfull = sem("c_dfull")
        c_dout = sem("c_dout")
        unsorted = [sem(f"unsorted{n}") for n in range(4)]
        final_in = [sem(f"final_in{n}") for n in range(NB)]
        final_mul = sem("final_mul")
        final_done = sem("final_done")
        stored = sem("stored")

        BT = bank[0:2]
        BQ = bank[2:4]
        BS = bank[4:6]
        BY = bank[6]
        BR = bank[7]
        logits = BR[:, 0:TILES * E].rearrange("p (j e) -> p j e", e=E)
        R0 = 256
        rank_ps = BR[:, R0:R0 + (TILES + 1) * E].rearrange("p (j e) -> p j e", e=E)

        def apart(eng, sem_, value):
            if not isinstance(value, int):
                value = eng.to_reg(value)
                eng.wait_ge(s_table, 16)
            eng.wait_ge(sem_, value)

        def batches(eng, step):
            for k in range(-1, NB + 1):
                step(At(k))

        def shared_batches(eng, step):
            for k in range(0, NB + 1):
                step(At(k))

        def blocks(eng, step):
            for k in range(-1, BLOCKS + 2):
                step(At(k, None, 4))

        def in_range(b, n):
            return b.i is not None or 0 <= b.k < n

        def layer_norm_turn(b, n):
            if n == 0:
                return b.count(2, -1) if b.k >= 2 else b.k + 1
            return b.count(2, 4) if b.i is not None else min(2 * b.k + 4, NB + 1 + b.k)

        block = ctx.enter_context(nc.Block())

        @block.sync
        def _(sp):
            sp.dma_start(tab[:, :], table).then_inc(s_table, 16)
            sp.dma_start(x_all[:, 0], x_tok[:, 0]).then_inc(s_x[0], 16)
            sp.dma_start(sel_sb[:, :, :], sel).then_inc(s_cond, 16)
            sp.dma_start(wmod_sb[:, :], wmod).then_inc(s_cond, 16)
            sp.dma_start(c_cols[:, :], c.rearrange("b d -> d b"), allow_slow_non_contiguous=True).then_inc(s_cond, 16)
            for n, w in enumerate((w_q, w_k, w_v)):
                for q in range(HEAD_D):
                    sp.dma_start(w_rep[q * HEADS:(q + 1) * HEADS, n],
                                 w[q].rearrange("d h -> (d h)").unsqueeze(0).broadcast_to([HEADS, D])
                                 ).then_inc(s_weights, 16)
            sp.dma_start(w_router[:, :], gate_w).then_inc(s_weights, 16)
            for b in range(1, NB):
                sp.dma_start(x_all[:, b], x_tok[:, b]).then_inc(s_x[1], 16)
            sp.dma_start(w_sgu[:, 0], sg_w).then_inc(s_shared_w, 16)
            sp.dma_start(w_sgu[:, 1], su_w).then_inc(s_shared_w, 16)
            sp.dma_start(w_sd[:, :, :], sd_w.rearrange("(c p) n -> p c n", p=P)).then_inc(s_shared_w, 16)
            sp.wait_ge(blank_made, 2)
            sp.dma_start(sorted_rows.rearrange("(b p) n -> p b n", p=P),
                         blank[:, :].unsqueeze(1).broadcast_to([P, BLOCKS, ROW])).then_inc(blank_kept, 16)
            for e in range(0, E, 8):
                sp.dma_start(w_gu[:, e:e + 8, 0:F], rg_w[e:e + 8].rearrange("e p n -> p e n")).then_inc(s_routed_w, 16)
                sp.dma_start(w_gu[:, e:e + 8, F:2 * F], ru_w[e:e + 8].rearrange("e p n -> p e n")).then_inc(s_routed_w, 16)

            def keep(b):
                bk, before = use_of("n2", b)
                sp.wait_ge(t_out[bk], before + 1)
                sp.dma_start(h2t_all[:, b.number], ht2[:, b.k % 2]).then_inc(h2t_kept[b.k % 2], 16)

            keep(At(0))
            with sp.Fori(0, (NB - 2) // 2) as i:
                keep(At(1, i))
                keep(At(2, i))
            keep(At(NB - 1))
            sp.wait_ge(rank_done, NB)
            for e in range(0, E, 8):
                sp.dma_start(w_down[:, e:e + 8], rd_w[e:e + 8].rearrange("e (c p) n -> p e c n", p=P)).then_inc(s_down_w, 16)

            def load_xs(b):
                if b.k >= 2:
                    sp.wait_ge(scattered[b.k % 2], b.turn(2, 16 * TILES, 0))
                sp.dma_start(xs_ring[:, b.k % 2, :, 0:D], xs_all[:, b.number]).then_inc(xs_in[b.k % 2], 16)

            for n in range(2):
                sp.wait_ge(t_out[n], USES_OF_BANK[n])
            load_xs(At(0))
            load_xs(At(1))
            with sp.Fori(0, (NB - 2) // 2) as i:
                load_xs(At(2, i))
                load_xs(At(3, i))

            for n in range(2):
                sp.wait_ge(scattered[n], 16 * TILES * NB // 2)

            def load_rows(b):
                if b.k >= 4:
                    sp.wait_ge(c_tfull, b.count(1, -3))
                    sp.wait_ge(ids_kept, b.count(1, -3))
                sp.dma_start(rows_in[:, b.k % 4], sorted_rows[bass.ds(b.count(P, 0), P), :]
                             ).then_inc(rows_in_s[b.k % 4], 16)

            for k in range(4):
                load_rows(At(k, None, 4))
            with sp.Fori(0, (BLOCKS - 7) // 4) as i:
                for k in range(4, 8):
                    load_rows(At(k, i, 4))
            for k in range(BLOCKS - 3, BLOCKS):
                load_rows(At(k, None, 4))

            for n in range(4):
                sp.wait_ge(unsorted[n], 16 * len(range(n, BLOCKS, 4)))
            for b in range(NB):
                sp.dma_start(base_tiles[:, b].rearrange("p (j d) -> p j d", j=TILES), routed_tok[:, b]
                             ).then_inc(final_in[b], 16)
            for b in range(NB):
                sp.wait_ge(final_done, b + 1)
                sp.dma_start(out_tok[:, b], x_all[:, b]).then_inc(stored, 16)
            sp.wait_ge(stored, 16 * NB)

        @block.gpsimd
        def _(pool):
            nc.gpsimd.memset(blank[:, :], 0.0).then_inc(blank_made, 1)
            pool.wait_ge(blank_made, 1)
            nc.gpsimd.iota(blank[:, D:ROW].bitcast(I32), [[0, 1]], base=TOKENS, channel_multiplier=1
                           ).then_inc(blank_made, 1)
            nc.gpsimd.iota(ids_all[:, :, :], [[T, NB], [P, TILES]], base=0, channel_multiplier=1).then_inc(ids_made, 1)
            nc.gpsimd.memset(minus_half[:, :], -0.5).then_inc(pool_consts, 1)
            pool.wait_ge(pool_consts, 1)

            def rstd_of(b, n):
                apart(pool, aggr_done, layer_norm_turn(b, n))
                nc.gpsimd.tensor_scalar(var_eps[:, n], mean_var[:, n, :, 1], EPS, None, ALU.add).then_inc(eps_done, 1)
                pool.wait_ge(eps_done, layer_norm_turn(b, n))
                nc.gpsimd.tensor_tensor(rstd[:, n], var_eps[:, n], minus_half[:, :], ALU.pow).then_inc(rstd_done, 1)

            def value_weights(b):
                if b.k >= 2:
                    apart(pool, q_full[1], b.count(2, -2))
                if b.k == 0:
                    pool.wait_ge(rows_out_done, 4)
                    pool.wait_ge(w_made, 4)
                nc.gpsimd.tensor_tensor(w_qkv[:, b.k % 2, 2 * D:3 * D], w_v_full[:, :],
                                        gate_rows[:, b.number, 0], ALU.mult).then_inc(wv_ready, 1)

            def rope(b, j):
                qk = qkv[:, b.k % 2, j, 0:2 * D].rearrange("p (q i two) -> p q i two", q=2, two=2)
                s = rope_s[:, j % 2].rearrange("p (q i two) -> p q i two", q=2, two=2)
                sine = sines[:, j].unsqueeze(1).broadcast_to([P, 2, D // 2])
                pool.wait_ge(q_out[j % 2], b.count(2, j // 2 + 1))
                if not (b.k == 0 and j < 2):
                    pool.wait_ge(rot_done, b.count(TILES, j - 1))
                nc.gpsimd.tensor_tensor(s[:, :, :, 0], qk[:, :, :, 1], sine, ALU.mult)
                nc.gpsimd.tensor_tensor(s[:, :, :, 1], qk[:, :, :, 0], sine, ALU.mult).then_inc(sin_done, 1)
                pool.wait_ge(sin_done, b.count(TILES, j + 1))
                pool.wait_ge(cos_done, b.count(TILES, j + 1))
                if b.k >= 1:
                    bk, before = use_of(f"qk{j // 2}", b + -1)
                    pool.wait_ge(t_full[bk], before + 1)
                r = rot[:, j].rearrange("p (q i two) -> p q i two", q=2, two=2)
                c_ = rope_c[:, j % 2].rearrange("p (q i two) -> p q i two", q=2, two=2)
                nc.gpsimd.tensor_tensor(r[:, :, :, 0], c_[:, :, :, 0], s[:, :, :, 0], ALU.subtract)
                nc.gpsimd.tensor_tensor(r[:, :, :, 1], c_[:, :, :, 1], s[:, :, :, 1], ALU.add).then_inc(rot_done, 1)

            def step(b):
                if in_range(b + 1, NB):
                    rstd_of(b + 1, 0)
                    value_weights(b + 1)
                if in_range(b + -1, NB):
                    rstd_of(b + -1, 1)
                if in_range(b + 1, NB):
                    for j in range(TILES):
                        rope(b + 1, j)

            batches(pool, step)

            pool.wait_ge(blank_kept, 16)
            pool.wait_ge(ids_made, 1)

            def scatter(b):
                r = b.k % 2
                if b.k == 0:
                    pool.wait_ge(pos_done, 1)
                if b.k >= 2:
                    apart(pool, scattered[r], b.turn(2, 16 * TILES, 0))
                nc.gpsimd.tensor_copy(pos_ring[:, r], pos_all[:, b.number]).then_inc(ids_in, 1)
                nc.gpsimd.tensor_copy(xs_ring[:, r, :, D].bitcast(I32), ids_all[:, b.number]).then_inc(ids_in, 1)
                apart(pool, ids_in, b.count(2, 2))
                apart(pool, xs_in[r], b.turn(2, 16, 16))
                for j in range(TILES):
                    nc.gpsimd.indirect_dma_start(
                        out=sorted_rows, out_offset=bass.IndirectOffsetOnAxis(ap=pos_ring[:, r, j:j + 1], axis=0),
                        in_=xs_ring[:, r, j], in_offset=None).then_inc(scattered[r], 16)

            scatter(At(0))
            scatter(At(1))
            with nc.gpsimd.Fori(0, (NB - 2) // 2) as i:
                scatter(At(2, i))
                scatter(At(3, i))

            def block_step(b):
                if in_range(b, BLOCKS):
                    r = b.k % 4
                    if b.k >= 4:
                        apart(pool, unsorted[r], b.turn(4, 16, 0))
                    apart(pool, rows_in_s[r], b.turn(4, 16, 16))
                    nc.gpsimd.tensor_copy(ids_out[:, r:r + 1], rows_in[:, r, D:ROW].bitcast(I32)).then_inc(ids_kept, 1)
                o = b + -2
                if in_range(o, BLOCKS):
                    r = o.k % 4
                    apart(pool, ids_kept, o.count(1, 1))
                    apart(pool, c_dout, o.count(1, 1))
                    nc.gpsimd.indirect_dma_start(
                        out=routed_rows, out_offset=bass.IndirectOffsetOnAxis(ap=ids_out[:, r:r + 1], axis=0),
                        in_=rows_out[:, r], in_offset=None, bounds_check=TOKENS - 1, oob_is_err=False).then_inc(unsorted[r], 16)

            blocks(nc.gpsimd, block_step)

        @block.tensor
        def _(pe):
            pe.wait_ge(s_cond, 48)
            pe.wait_ge(c_step, 3)
            for n, part in enumerate((0, 1, 3, 4)):
                nc.tensor.matmul(BR[:, n * NB:(n + 1) * NB], wmod_sb[:, part * D:(part + 1) * D], c_silu[:, :],
                                 start=True, stop=True)
            for n, part in enumerate((2, 5)):
                last = nc.tensor.matmul(BY[0:NB, n * D:(n + 1) * D], c_silu[:, :], wmod_sb[:, part * D:(part + 1) * D],
                                        start=True, stop=True)
            last.then_inc(mod_full, 1)
            pe.wait_ge(g_step, G_STEPS)
            for b in range(NB):
                last = nc.tensor.matmul(bank[b // 2][:, (b % 2) * 2 * D:(b % 2 + 1) * 2 * D], sel_sb[:, b], g_rows[:, :],
                                        start=True, stop=True)
                if b % 2:
                    last.then_inc(rows_full, 1)
            pe.wait_ge(rows_out_done, 4)
            pe.wait_ge(mod_out, 2)
            pe.wait_ge(consts_made, CONSTS)
            pe.wait_ge(w_made, 4)

            def bank_for(kind, b):
                bk, before = use_of(kind, b)
                if not isinstance(before, int) or before:
                    pe.wait_ge(t_out[bk], before)
                return BT[bk], t_full[bk]

            def read_out(kind, b):
                bk, before = use_of(kind, b)
                pe.wait_ge(t_out[bk], before + 1)

            def normed_t(b):
                pe.wait_ge(norm1_done, b.count(1, 1))
                to, full = bank_for("n1", b)
                for j in range(TILES):
                    last = nc.tensor.transpose(to[:, j * P:(j + 1) * P], normed[:, b.k % 2, j], ident)
                last.then_inc(full, 1)

            def project(b, j):
                if j == 0:
                    read_out("n1", b)
                    pe.wait_ge(wv_ready, b.count(1, 1))
                if not (b.k == 0 and j < 2):
                    pe.wait_ge(q_out[j % 2], b.count(2, j // 2))
                nc.tensor.matmul(BQ[j % 2][:, 0:3 * D], ht[:, b.k % 2, j * P:(j + 1) * P], w_qkv[:, b.k % 2],
                                 start=True, stop=True).then_inc(q_full[j % 2], 1)

            def rotated_t(b, half):
                pe.wait_ge(rot_done, b.count(TILES, 2 * half + 2))
                to, full = bank_for(f"qk{half}", b)
                for q in range(2):
                    for j in range(2):
                        last = nc.tensor.transpose(to[:, (2 * q + j) * P:(2 * q + j + 1) * P],
                                                   rot[:, 2 * half + j, q * D:(q + 1) * D], ident)
                last.then_inc(full, 1)

            def scores(b, j):
                if j == 0:
                    read_out("qk0", b)
                    read_out("qk1", b)
                if not (b.k == 0 and j < 2):
                    pe.wait_ge(exp_done, b.count(TILES, j - 1))
                nc.tensor.matmul(BS[j % 2][:, 0:(j + 1) * P], qkt[:, 0, j * P:(j + 1) * P], qkt[:, 1, 0:(j + 1) * P],
                                 start=True, stop=True)
                nc.tensor.matmul(BS[j % 2][:, j * P:(j + 1) * P], ident_b[:, :], mask_b[:, :],
                                 start=False, stop=True, skip_group_check=True).then_inc(s_full, 1)

            def probs_turned(b, j):
                pe.wait_ge(exp_done, b.count(TILES, j + 1))
                to, full = bank_for(f"p{j}", b)
                for k in range(j + 1):
                    last = nc.tensor.transpose(to[:, k * P:(k + 1) * P], probs[:, j % 2, k * P:(k + 1) * P], ident)
                last.then_inc(full, 1)

            def values(b, j):
                read_out(f"p{j}", b)
                if j == 0 and b.k > 0:
                    pe.wait_ge(x2_done, b.count(1, 0))
                for k in range(j + 1):
                    last = nc.tensor.matmul(BY[:, j * D:(j + 1) * D], probs_t[:, j % 2, k],
                                            qkv[:, b.k % 2, k, 2 * D:3 * D], start=(k == 0), stop=(k == j))
                last.then_inc(y_full, 1)

            def second_t(b):
                pe.wait_ge(norm2_done, b.count(1, 1))
                to, full = bank_for("n2", b)
                for j in range(TILES):
                    last = nc.tensor.transpose(to[:, j * P:(j + 1) * P], normed2[:, j], ident)
                last.then_inc(full, 1)

            def route(b):
                read_out("n2", b)
                pe.wait_ge(rank_step, b.count(2, 1))
                for j in range(TILES):
                    last = nc.tensor.matmul(logits[:, j], ht2[:, b.k % 2, j * P:(j + 1) * P], w_router[:, :],
                                            start=True, stop=True)
                last.then_inc(r_full, 1)

            def rows_again(b):
                to, full = bank_for("h2", b)
                for j in range(TILES):
                    last = nc.tensor.transpose(to[:, j * P:(j + 1) * P], ht2[:, b.k % 2, j * P:(j + 1) * P], ident)
                last.then_inc(full, 1)

            def rank(b):
                pe.wait_ge(onehot_done, b.count(1, 1))
                nc.tensor.matmul(rank_ps, upper_b[:, :], onehot[:, b.number], start=True, stop=True)
                for j in range(TILES):
                    last = nc.tensor.matmul(rank_ps[:, j + 1:], ones_b[:, :],
                                            onehot[:, b.number, j:j + 1].broadcast_to([P, TILES - j, E]),
                                            start=False, stop=True, skip_group_check=True)
                last.then_inc(r_full, 1)

            def step(b):
                now, nxt, prev = in_range(b, NB), in_range(b + 1, NB), in_range(b + -1, NB)
                if now:
                    rotated_t(b, 0)
                    rotated_t(b, 1)
                    scores(b, 0)
                    scores(b, 1)
                if nxt:
                    normed_t(b + 1)
                if now:
                    probs_turned(b, 0)
                    scores(b, 2)
                    probs_turned(b, 1)
                if nxt:
                    project(b + 1, 0)
                if now:
                    values(b, 0)
                    scores(b, 3)
                if nxt:
                    project(b + 1, 1)
                if prev:
                    second_t(b + -1)
                if now:
                    values(b, 1)
                    probs_turned(b, 2)
                if nxt:
                    project(b + 1, 2)
                if prev:
                    route(b + -1)
                if now:
                    values(b, 2)
                if nxt:
                    project(b + 1, 3)
                if now:
                    probs_turned(b, 3)
                if prev:
                    rows_again(b + -1)
                if now:
                    values(b, 3)
                if prev:
                    rank(b + -1)

            batches(nc.tensor, step)

            pe.wait_ge(s_shared_w, 48)
            pe.wait_ge(rank_step, 2 * NB + 2)
            for n in range(2):
                pe.wait_ge(t_out[n], USES_OF_BANK[n])
            for n in range(2):
                pe.wait_ge(h2t_kept[n], 16 * NB // 2)

            def shared_up(b):
                for ch in range(FC):
                    for gu in range(2):
                        if b.k > 0:
                            pe.wait_ge(act_done if gu else silu_done, b.count(FC, ch + 1 - FC))
                        nc.tensor.matmul(bank[2 * ch + gu][:, :], w_sgu[:, gu, ch * P:(ch + 1) * P],
                                         h2t_all[:, b.number], start=True, stop=True).then_inc(gu_full, 1)

            def shared_down(b):
                pe.wait_ge(act_done, b.count(FC, FC))
                for j in range(TILES):
                    for ch in range(FC):
                        last = nc.tensor.matmul(bank[4 + b.k % 2][:, j * D:(j + 1) * D],
                                                sh_act_t[:, b.k % 2, ch, j * P:(j + 1) * P], w_sd[:, ch],
                                                start=(ch == 0), stop=(ch == FC - 1))
                last.then_inc(d_full, 1)

            def shared_step(b):
                if in_range(b, NB):
                    shared_up(b)
                if b.k == NB - 1:
                    pe.wait_ge(sort_step, SORT_STEPS)
                    nc.tensor.matmul(BR[0:1, 0:P], expert_col[:, :], ident, start=True, stop=True).then_inc(expert_full, 1)
                if in_range(b + -1, NB):
                    shared_down(b + -1)

            shared_batches(nc.tensor, shared_step)

            pe.wait_ge(s_routed_w, 16 * 2 * E // 8)
            pe.wait_ge(s_down_w, 16 * E // 8)
            pe.wait_ge(expert_done, 1)
            pe.wait_ge(base_done, NB + 1)

            def rows_turned(b):
                pe.wait_ge(rows_in_s[b.k % 4], b.turn(4, 16, 16))
                if b.k >= 2:
                    pe.wait_ge(c_tout, b.count(1, -1))
                nc.tensor.transpose(bank[b.k % 2][:, 0:P], rows_in[:, b.k % 4, 0:D], ident).then_inc(c_tfull, 1)

            at = {}

            def experts_of(k):
                n = min(BLOCKS_PER_LOAD, BLOCKS - k)
                _, values = nc.values_load_multi_w_load_instructions(
                    expert_row[0:1, k:k + n], engines=[mybir.EngineType.PE], min_val=0, max_val=(E - 1) * FC * D,
                    skip_runtime_bounds_check_because="DVE counts at most E experts and takes the minimum with E - 1")
                for m, value in enumerate(values):
                    at[k + m] = value

            def expert_up(b):
                pe.wait_ge(c_tout, b.count(1, 1))
                if b.k >= 2:
                    pe.wait_ge(c_act, b.count(1, -1))
                nc.tensor.matmul(bank[2 + b.k % 2][:, :], rows_t[:, b.k % 2], 
                                 w_gu_flat[:, bass.ds(at[b.k] * (2 * F // (FC * D)), 2 * F)], start=True, stop=True).then_inc(c_gfull, 1)

            def act_turned(b):
                pe.wait_ge(c_act, b.count(1, 1))
                if b.k >= 2:
                    pe.wait_ge(c_aout, b.count(1, -1))
                for ch in range(FC):
                    last = nc.tensor.transpose(bank[4 + b.k % 2][:, ch * P:(ch + 1) * P],
                                               r_act[:, b.k % 2, ch * P:(ch + 1) * P], ident)
                last.then_inc(c_afull, 1)

            def expert_down(b):
                pe.wait_ge(c_aout, b.count(1, 1))
                if b.k >= 2:
                    pe.wait_ge(c_dout, b.count(1, -1))
                for ch in range(FC):
                    last = nc.tensor.matmul(bank[6 + b.k % 2][:, 0:D], r_act_t[:, b.k % 2, ch],
                                            w_down_flat[:, bass.ds(at[b.k] + ch * D, D)],
                                            start=(ch == 0), stop=(ch == FC - 1))
                last.then_inc(c_dfull, 1)

            def block_step(b):
                if in_range(b + 1, BLOCKS):
                    rows_turned(b + 1)
                if in_range(b, BLOCKS):
                    if b.k % BLOCKS_PER_LOAD == 0:
                        experts_of(b.k)
                    expert_up(b)
                if in_range(b + -2, BLOCKS):
                    expert_down(b + -2)
                if in_range(b + -1, BLOCKS):
                    act_turned(b + -1)

            blocks(nc.tensor, block_step)

        @block.scalar
        def _(act):
            act.wait_ge(s_cond, 48)
            nc.scalar.activation(c_exp[:, :], c_cols[:, :], ACT.Exp, scale=-1.0).then_inc(c_exp_done, 1)
            for n in range(4):
                act.wait_ge(rows_full, n + 1)
                nc.scalar.copy(gate_rows[:, 2 * n:2 * n + 2].rearrange("p b g d -> p (b g d)"), bank[n][:, :]
                               ).then_inc(rows_out_done, 1)

            def full(kind, b, indexed=False):
                bk, before = use_of(kind, b)
                if indexed:
                    apart(act, t_full[bk], before + 1)
                else:
                    act.wait_ge(t_full[bk], before + 1)
                return BT[bk], t_out[bk]

            def rotated_out(b, half):
                frm, done = full(f"qk{half}", b)
                nc.scalar.copy(qkt[:, :, half * 2 * P:(half + 1) * 2 * P], frm[:, :].rearrange("p (q t) -> p q t", q=2)
                               ).then_inc(done, 1)

            def modulated_out(b, kind, dest, n):
                frm, done = full(kind, b, indexed=True)
                nc.scalar.activation(dest[:, b.k % 2], frm[:, :], ACT.Identity,
                                     bias=mod_cols[:, n, bass.ds(b.number, 1)],
                                     scale=mod_cols[:, n + 1, bass.ds(b.number, 1)]).then_inc(done, 1)

            def exponentials(b, j):
                act.wait_ge(max_done, b.count(TILES, j + 1))
                kind, of = (f"p{j - 2}", b) if j >= 2 else (f"p{j + 2}", b + -1)
                if of.k >= 0:
                    bk, before = use_of(kind, of)
                    act.wait_ge(t_full[bk], before + 1)
                nc.scalar.activation(probs[:, j % 2, 0:(j + 1) * P], BS[j % 2][:, 0:(j + 1) * P], ACT.Exp,
                                     bias=neg_max[:, j:j + 1], scale=1.0,
                                     accum_out=row_sum[:, b.k % 2, j:j + 1]).then_inc(exp_done, 1)

            def project_out(b, j):
                act.wait_ge(q_full[j % 2], b.count(2, j // 2 + 1))
                if j == 0 and b.k >= 2:
                    act.wait_ge(y_full, b.count(TILES, -TILES))
                nc.scalar.copy(qkv[:, b.k % 2, j], BQ[j % 2][:, 0:3 * D]).then_inc(q_out[j % 2], 1)

            def probs_out(b, j):
                frm, done = full(f"p{j}", b)
                act.wait_ge(y_full, b.count(TILES, j - 1))
                nc.scalar.copy(probs_t[:, j % 2, 0:j + 1], frm[:, 0:(j + 1) * P].rearrange("p (k t) -> p k t", t=P)
                               ).then_inc(done, 1)

            def second_out(b):
                modulated_out(b, "n2", ht2, 2)

            def sigmoid_exp(b):
                act.wait_ge(top_done, b.count(1, 1))
                nc.scalar.activation(top_exp[:, b.k % 2], top_logit[:, b.k % 2], ACT.Exp, scale=-1.0).then_inc(sig_exp, 1)

            def scaled_out(b):
                frm, done = full("h2", b, indexed=True)
                apart(act, score_done, b.count(1, 1))
                for j in range(TILES):
                    last = nc.scalar.activation(xs_all[:, b.number, j], frm[:, j * P:(j + 1) * P], ACT.Copy,
                                                scale=score[:, b.k % 2, j:j + 1])
                last.then_inc(done, 1)
                act.wait_ge(h2t_kept[b.k % 2], b.turn(2, 16, 16))

            def step(b):
                now, nxt, prev = in_range(b, NB), in_range(b + 1, NB), in_range(b + -1, NB)
                if now:
                    rotated_out(b, 0)
                    rotated_out(b, 1)
                if now:
                    exponentials(b, 0)
                if nxt:
                    modulated_out(b + 1, "n1", ht, 0)
                if now:
                    exponentials(b, 1)
                    exponentials(b, 2)
                if nxt:
                    project_out(b + 1, 0)
                if now:
                    exponentials(b, 3)
                if nxt:
                    project_out(b + 1, 1)
                if prev:
                    second_out(b + -1)
                if now:
                    probs_out(b, 2)
                if nxt:
                    project_out(b + 1, 2)
                    project_out(b + 1, 3)
                if now:
                    probs_out(b, 3)
                if prev:
                    sigmoid_exp(b + -1)
                    scaled_out(b + -1)

            act.wait_ge(mod_out, 2)
            batches(nc.scalar, step)

            def shared_silu(b):
                for ch in range(FC):
                    act.wait_ge(gu_full, b.count(2 * FC, 2 * ch + 1))
                    if b.k > 0:
                        act.wait_ge(act_done, b.count(FC, ch + 1 - FC))
                    nc.scalar.activation(sh_silu[:, ch], bank[2 * ch][:, :], ACT.Silu).then_inc(silu_done, 1)

            shared_silu(At(0))
            with nc.scalar.Fori(0, (NB - 2) // 2) as i:
                shared_silu(At(1, i))
                shared_silu(At(2, i))
            shared_silu(At(NB - 1))

            def block_step(b):
                n = b + 1
                if in_range(n, BLOCKS):
                    act.wait_ge(c_tfull, n.count(1, 1))
                    if n.k >= 2:
                        act.wait_ge(c_gfull, n.count(1, -1))
                    nc.scalar.copy(rows_t[:, n.k % 2], bank[n.k % 2][:, 0:P]).then_inc(c_tout, 1)
                if in_range(b, BLOCKS):
                    act.wait_ge(c_gfull, b.count(1, 1))
                    if b.k >= 2:
                        act.wait_ge(c_act, b.count(1, -1))
                    nc.scalar.activation(r_silu[:, b.k % 2], bank[2 + b.k % 2][:, 0:F], ACT.Silu).then_inc(c_silu_done, 1)
                o = b + -2
                if in_range(o, BLOCKS):
                    act.wait_ge(c_dfull, o.count(1, 1))
                    if o.k >= 4:
                        act.wait_ge(unsorted[o.k % 4], o.turn(4, 16, 0))
                    nc.scalar.copy(rows_out[:, o.k % 4], bank[6 + o.k % 2][:, 0:D]).then_inc(c_dout, 1)

            blocks(nc.scalar, block_step)

        @block.vector
        def _(dve):
            V = nc.vector
            dve.wait_ge(s_table, 16)
            V.tensor_copy(ident_b[:, :], ident).then_inc(consts_made, 1)
            V.tensor_copy(upper_b[:, :], tab[:, C_UP:C_UP + P]).then_inc(consts_made, 1)
            V.tensor_copy(mask_b[:, :], tab[:, C_MASK:C_MASK + P]).then_inc(consts_made, 1)
            V.memset(ones_b[:, :], 1.0).then_inc(consts_made, 1)
            V.memset(onehot[:, :, TILES], 0.0).then_inc(consts_made, 1)
            V.memset(ends[:, :, 0:PAD], 0.0).then_inc(consts_made, 1)
            V.memset(ranks[:, 1, TILES], 0.0).then_inc(rank_step, 1)
            V.memset(own_rank[:, :, :], 0.0).then_inc(rank_step, 1)
            V.memset(sh_gated[:, :, :], 0.0).then_inc(base_done, 1)
            dve.wait_ge(consts_made, CONSTS)
            dve.wait_ge(c_exp_done, 1)
            V.tensor_scalar(c_den[:, :], c_exp[:, :], 1.0, None, ALU.add).then_inc(c_step, 1)
            dve.wait_ge(c_step, 1)
            V.reciprocal(c_inv[:, :], c_den[:, :]).then_inc(c_step, 1)
            dve.wait_ge(c_step, 2)
            V.tensor_tensor(c_silu[:, :], c_cols[:, :], c_inv[:, :], ALU.mult).then_inc(c_step, 1)
            dve.wait_ge(s_weights, 16 * (3 * HEAD_D + 1))
            head = tab[:, C_HEAD:C_HEAD + D]
            V.scalar_tensor_tensor(out=w_qkv[:, 0, 0:D], in0=w_rep[:, 0], scalar=GAMMA, in1=head,
                                   op0=ALU.mult, op1=ALU.mult).then_inc(w_made, 1)
            V.tensor_tensor(w_qkv[:, 0, D:2 * D], w_rep[:, 1], head, ALU.mult).then_inc(w_made, 1)
            V.tensor_tensor(w_v_full[:, :], w_rep[:, 2], head, ALU.mult).then_inc(w_made, 1)
            dve.wait_ge(w_made, 3)
            V.tensor_copy(w_qkv[:, 1, 0:2 * D], w_qkv[:, 0, 0:2 * D]).then_inc(w_made, 1)
            dve.wait_ge(mod_full, 1)
            cols = BR[:, 0:4 * NB].rearrange("p (a two b) -> p a two b", two=2, b=NB)
            kept = mod_cols[:, :, :].rearrange("p (a two) b -> p a two b", two=2)
            V.tensor_copy(kept[:, :, 0], cols[:, :, 0]).then_inc(mod_out, 1)
            V.tensor_scalar(kept[:, :, 1], cols[:, :, 1], 1.0, None, ALU.add).then_inc(mod_out, 1)
            g = BY[0:NB, 0:2 * D]
            V.tensor_scalar(g_sign[:, :], g, 0.0, 2.0, ALU.is_ge, ALU.mult).then_inc(g_step, 1)
            V.tensor_copy(g_abs[:, :], g).then_inc(g_step, 1)
            dve.wait_ge(g_step, 2)
            V.scalar_tensor_tensor(out=g_rows[:, :], in0=g_abs[:, :], scalar=-1.0, in1=g_abs[:, :],
                                   op0=ALU.mult, op1=ALU.max).then_inc(g_step, 1)
            dve.wait_ge(g_step, 3)
            V.tensor_scalar(g_abs[:, :], g_rows[:, :], FLOOR, None, ALU.max).then_inc(g_step, 1)
            dve.wait_ge(g_step, 4)
            V.scalar_tensor_tensor(out=g_rows[:, :], in0=g_sign[:, :], scalar=1.0, in1=g_abs[:, :],
                                   op0=ALU.subtract, op1=ALU.mult).then_inc(g_step, 1)

            def statistics(b, n):
                if n == 0 and b.k == 0:
                    dve.wait_ge(s_x[0], 16)
                if n == 0 and b.k == 1:
                    dve.wait_ge(s_x[1], 16 * (NB - 1))
                if n == 1:
                    apart(dve, x2_done, b.count(1, 1))
                for j in range(TILES):
                    last = V.bn_stats(stats[:, n, j], x_all[:, b.number, j])
                last.then_inc(stat_done, 1)
                apart(dve, stat_done, layer_norm_turn(b, n))
                for j in range(TILES):
                    last = V.bn_aggr(mean_var[:, n, j], stats[:, n, j])
                last.then_inc(aggr_done, 1)

            def normalise(b, n):
                dve.wait_ge(rstd_done, layer_norm_turn(b, n))
                if n == 0 and b.k >= 2:
                    bk, before = use_of("n1", b + -2)
                    dve.wait_ge(t_full[bk], before + 1)
                for j in range(TILES):
                    dest = normed2[:, j] if n else normed[:, b.k % 2, j]
                    last = V.tensor_scalar(dest, x_all[:, b.number, j], mean_var[:, n, j, 0:1], rstd[:, n, j:j + 1],
                                           ALU.subtract, ALU.mult)
                last.then_inc(norm2_done if n else norm1_done, 1)

            def cosine_part(b, j):
                dve.wait_ge(q_out[j % 2], b.count(2, j // 2 + 1))
                if not (b.k == 0 and j < 2):
                    dve.wait_ge(rot_done, b.count(TILES, j - 1))
                V.tensor_tensor(rope_c[:, j % 2].rearrange("p (q d) -> p q d", q=2),
                                qkv[:, b.k % 2, j, 0:2 * D].rearrange("p (q d) -> p q d", q=2),
                                cosines[:, j].unsqueeze(1).broadcast_to([P, 2, D]), ALU.mult).then_inc(cos_done, 1)

            def row_max(b, j):
                dve.wait_ge(s_full, b.count(TILES, j + 1))
                if b.k > 0:
                    dve.wait_ge(exp_done, b.count(TILES, j + 1 - TILES))
                V.tensor_reduce(neg_max[:, j:j + 1], BS[j % 2][:, 0:(j + 1) * P], AX.X, ALU.max, negate=True
                                ).then_inc(max_done, 1)

            def probs_out(b, j):
                bk, before = use_of(f"p{j}", b)
                dve.wait_ge(t_full[bk], before + 1)
                if b.k > 0:
                    dve.wait_ge(y_full, b.count(TILES, j + 3 - TILES))
                V.tensor_copy(probs_t[:, j % 2, 0:j + 1], BT[bk][:, 0:(j + 1) * P].rearrange("p (k t) -> p k t", t=P)
                              ).then_inc(t_out[bk], 1)

            def attention_out(b):
                dve.wait_ge(y_full, b.count(TILES, TILES))
                V.reciprocal(row_inv[:, :], row_sum[:, b.k % 2]).then_inc(inv_done, 1)
                apart(dve, inv_done, b.count(1, 1))
                for j in range(TILES):
                    last = V.scalar_tensor_tensor(out=x_all[:, b.number, j], in0=BY[:, j * D:(j + 1) * D],
                                                  scalar=row_inv[:, j:j + 1], in1=x_all[:, b.number, j],
                                                  op0=ALU.mult, op1=ALU.add)
                last.then_inc(x2_done, 1)

            def choose(b):
                dve.wait_ge(r_full, b.count(2, 1))
                V.tensor_reduce(top_logit[:, b.k % 2], logits, AX.X, ALU.max).then_inc(top_done, 1)
                dve.wait_ge(top_done, b.count(1, 1))
                V.tensor_tensor(tied[:, :, :], logits, top_logit[:, b.k % 2].unsqueeze(2).broadcast_to([P, TILES, E]),
                                ALU.is_equal).then_inc(r_step, 1)
                dve.wait_ge(r_step, b.count(3, 1))
                V.tensor_tensor(tied[:, :, :], tied[:, :, :], reversed_e.unsqueeze(1).broadcast_to([P, TILES, E]),
                                ALU.mult).then_inc(r_step, 1)
                dve.wait_ge(r_step, b.count(3, 2))
                V.tensor_reduce(first[:, :], tied[:, :, :], AX.X, ALU.max).then_inc(r_step, 1)
                dve.wait_ge(r_step, b.count(3, 3))
                V.tensor_tensor(onehot[:, b.number, 0:TILES], first[:, :].unsqueeze(2).broadcast_to([P, TILES, E]),
                                reversed_e.unsqueeze(1).broadcast_to([P, TILES, E]), ALU.is_equal
                                ).then_inc(onehot_done, 1)

            def score_of(b):
                dve.wait_ge(sig_exp, b.count(1, 1))
                V.tensor_scalar(top_den[:, :], top_exp[:, b.k % 2], 1.0, None, ALU.add).then_inc(g_step, 1)
                dve.wait_ge(g_step, b.count(1, G_STEPS + 1))
                V.reciprocal(score[:, b.k % 2], top_den[:, :]).then_inc(score_done, 1)

            def ranks_out(b):
                dve.wait_ge(r_full, b.count(2, 2))
                V.tensor_tensor(ranks[:, b.k % 2], rank_ps,
                                ranks[:, (b.k + 1) % 2, TILES:TILES + 1].broadcast_to([P, TILES + 1, E]), ALU.add
                                ).then_inc(rank_step, 1)
                dve.wait_ge(rank_step, b.count(2, 3))
                V.tensor_tensor(own_rank[:, :, :], ranks[:, b.k % 2, 0:TILES], onehot[:, b.number, 0:TILES], ALU.mult
                                ).then_inc(rank_step, 1)
                apart(dve, rank_step, b.count(2, 4))
                V.tensor_reduce(rank_all[:, b.number], own_rank[:, :, :], AX.X, ALU.add).then_inc(rank_done, 1)

            def step(b):
                now, nxt, prev = in_range(b, NB), in_range(b + 1, NB), in_range(b + -1, NB)
                if nxt:
                    statistics(b + 1, 0)
                if prev:
                    attention_out(b + -1)
                if now:
                    row_max(b, 0)
                if nxt:
                    normalise(b + 1, 0)
                if now:
                    row_max(b, 1)
                if prev:
                    statistics(b + -1, 1)
                if now:
                    probs_out(b, 0)
                    row_max(b, 2)
                if prev:
                    normalise(b + -1, 1)
                if now:
                    probs_out(b, 1)
                if nxt:
                    cosine_part(b + 1, 0)
                if now:
                    row_max(b, 3)
                if nxt:
                    cosine_part(b + 1, 1)
                    cosine_part(b + 1, 2)
                if prev:
                    choose(b + -1)
                if nxt:
                    cosine_part(b + 1, 3)
                if prev:
                    score_of(b + -1)
                    ranks_out(b + -1)

            batches(V, step)

            steps = [0]

            def chained(ins):
                steps[0] += 1
                ins.then_inc(sort_step, 1)
                dve.wait_ge(sort_step, steps[0])

            dve.wait_ge(rank_done, NB)
            counts = ranks[:, (NB - 1) % 2, TILES]
            chained(V.tensor_scalar(n_pad[:, :], counts, float(P - 1), None, ALU.add))
            chained(V.tensor_scalar(n_blocks[:, :], n_pad[:, :], P.bit_length() - 1, None, ALU.arith_shift_right))
            chained(V.tensor_copy(ends[:, 0, PAD:], n_blocks[:, :]))
            shift, cur = 1, 0
            while shift < E:
                chained(V.tensor_tensor(ends[:, 1 - cur, PAD:], ends[:, cur, PAD:], ends[:, cur, PAD - shift:PAD + E - shift],
                                        ALU.add))
                shift, cur = 2 * shift, 1 - cur
            chained(V.tensor_scalar(before_me[:, :], ends[:, cur, PAD:], row_number, None, ALU.is_le))
            chained(V.tensor_reduce(expert_col[:, :], before_me[:, :], AX.X, ALU.add))
            assert steps[0] == SORT_STEPS
            chained(V.tensor_tensor(base[:, :], ends[:, cur, PAD:], n_blocks[:, :], ALU.subtract))
            chained(V.tensor_tensor(base_wide, onehot[:, :, 0:TILES],
                                    base[:, :].unsqueeze(1).unsqueeze(1).broadcast_to([P, NB, TILES, E]), ALU.mult))
            chained(V.tensor_reduce(base_own[:, :], base_wide.rearrange("p b j e -> p (b j) e"), AX.X, ALU.add))
            V.scalar_tensor_tensor(out=pos_all[:, :, :].rearrange("p b j -> p (b j)"), in0=base_own[:, :], scalar=float(P),
                                   in1=rank_all[:, :, :].rearrange("p b j -> p (b j)"), op0=ALU.mult, op1=ALU.add
                                   ).then_inc(pos_done, 1)

            def shared_act(b):
                for ch in range(FC):
                    dve.wait_ge(silu_done, b.count(FC, ch + 1))
                    dve.wait_ge(gu_full, b.count(2 * FC, 2 * ch + 2))
                    V.tensor_tensor(sh_act_t[:, b.k % 2, ch], sh_silu[:, ch], bank[2 * ch + 1][:, :], ALU.mult
                                    ).then_inc(act_done, 1)

            def shared_base(b):
                dve.wait_ge(d_full, b.count(1, 1))
                dve.wait_ge(base_done, b.count(1, 1))
                V.tensor_tensor(sh_gated[:, :, :], bank[4 + b.k % 2][:, :].rearrange("p (j d) -> p j d", j=TILES),
                                gate_rows[:, b.number, 1:2].broadcast_to([P, TILES, D]), ALU.mult).then_inc(gated, 1)
                dve.wait_ge(gated, b.count(1, 1))
                V.tensor_tensor(x_all[:, b.number], x_all[:, b.number], sh_gated[:, :, :], ALU.add).then_inc(base_done, 1)

            def shared_step(b):
                if in_range(b, NB):
                    shared_act(b)
                if b.k == NB - 1:
                    dve.wait_ge(expert_full, 1)
                    V.tensor_scalar(expert_row[:, :], BR[0:1, 0:P], float(E - 1), float(FC * D), ALU.min, ALU.mult).then_inc(expert_done, 1)
                if in_range(b + -1, NB):
                    shared_base(b + -1)

            shared_batches(V, shared_step)

            def block_step(b):
                if in_range(b, BLOCKS):
                    dve.wait_ge(c_silu_done, b.count(1, 1))
                    if b.k >= 2:
                        dve.wait_ge(c_afull, b.count(1, -1))
                    V.tensor_tensor(r_act[:, b.k % 2], r_silu[:, b.k % 2], bank[2 + b.k % 2][:, F:2 * F], ALU.mult
                                    ).then_inc(c_act, 1)
                o = b + -1
                if in_range(o, BLOCKS):
                    dve.wait_ge(c_afull, o.count(1, 1))
                    if o.k >= 2:
                        dve.wait_ge(c_dfull, o.count(1, -1))
                    V.tensor_copy(r_act_t[:, o.k % 2], bank[4 + o.k % 2][:, 0:F].rearrange("p (c t) -> p c t", c=FC)
                                  ).then_inc(c_aout, 1)

            blocks(V, block_step)

            for b in range(NB):
                dve.wait_ge(final_in[b], 16)
                rows = base_tiles[:, b].rearrange("p (j d) -> p j d", j=TILES)
                V.tensor_tensor(rows, rows, gate_rows[:, b, 1:2].broadcast_to([P, TILES, D]), ALU.mult
                                ).then_inc(final_mul, 1)
                dve.wait_ge(final_mul, b + 1)
                V.tensor_tensor(x_all[:, b], x_all[:, b], rows, ALU.add).then_inc(final_done, 1)


_INS = ["L0_attn_x", "L0_attn_w_q", "L0_attn_w_k", "L0_attn_w_v", "L0_ffn_gate_w", "L0_ffn_shared_gate_w",
        "L0_ffn_shared_up_w", "L0_ffn_shared_down_w", "L0_ffn_routed_gate_w", "L0_ffn_routed_up_w",
        "L0_ffn_routed_down_w", "L0_c", "L0_wmod"]


def constants():
    import numpy as np

    n = np.arange(P)
    table = np.zeros((P, C_ALL), np.float32)
    table[:, C_ID:C_ID + P] = np.eye(P)
    table[:, C_UP:C_UP + P] = n[:, None] < n[None, :]
    table[:, C_MASK:C_MASK + P] = np.where(n[None, :] > n[:, None], np.float32(-3e38), np.float32(0))
    table[:, C_HEAD:C_HEAD + D] = n[:, None] % HEADS == n[None, :] % HEADS
    half = D // 2
    inv_freq = (np.float32(1.0) / np.float32(10000.0) ** (np.arange(half, dtype=np.float32) / np.float32(half)))
    angle = np.arange(T, dtype=np.float32)[:, None] * inv_freq.astype(np.float32)[None, :]
    cos = np.cos(angle).reshape(TILES, P, half).transpose(1, 0, 2)
    sin = np.sin(angle).reshape(TILES, P, half).transpose(1, 0, 2)
    table[:, C_COS:C_SIN] = np.repeat(cos, 2, axis=2).reshape(P, TILES * D)
    table[:, C_SIN:C_REV] = sin.reshape(P, TILES * half)
    table[:, C_REV:C_REV + E] = E - np.arange(E)
    table[:, C_ROW] = n
    sel = np.zeros((NB, NB, P), np.float32)
    for b in range(NB):
        sel[b, b] = 1.0
    return table, sel


def kernel(**inputs):
    import numpy as _np
    import concourse.bacc as _bacc
    from concourse import mybir as _mybir
    from concourse.bass_utils import run_bass_kernel_spmd as _run

    nc = _bacc.Bacc("TRN2", target_bir_lowering=False, num_devices=1)
    table, sel = constants()
    arrays, args = {}, []
    for name, a in [(n, _np.ascontiguousarray(inputs[n])) for n in _INS] + [("table", table), ("sel", sel)]:
        arrays[f"in_{name}"] = a
        args.append(nc.dram_tensor(f"in_{name}", a.shape, _mybir.dt.from_np(a.dtype), kind="ExternalInput").ap())
    args.append(nc.dram_tensor("out_0", (NB, T, D), F32, kind="ExternalOutput").ap())
    block_program(nc, *args)
    r = _run(nc, [arrays], core_ids=[0])
    return r.results[0]["out_0"]
```

```python
from contextlib import ExitStack

import concourse.bass as bass
from concourse import mybir

F32 = mybir.dt.float32
BF16 = mybir.dt.bfloat16
I32 = mybir.dt.int32
ALU = mybir.AluOpType
ACT = mybir.ActivationFunctionType
AX = mybir.AxisListType

P = 128
D = 128
NB = 8
T = 512
TILES = T // P
HEADS = 16
HEAD_D = D // HEADS
E = 32
F = 256
FC = F // P
TOKENS = NB * T
BLOCKS = (TOKENS - E) // P + E
PARTS = [0, E + (BLOCKS - E) // 2 // 8 * 8 + 8, BLOCKS - (BLOCKS - E) // 4, BLOCKS]
BLOCKS_PER_LOAD = 8
POOL_SUMS = [3, 6]
DVE_SUMS = [b for b in range(NB) if b not in POOL_SUMS]
CAP = TOKENS + P
ROW = D + 1
GAMMA = float(D) ** -0.5
EPS = 1e-5
FLOOR = 0.25

C_ID, C_UP, C_MASK, C_HEAD = 0, P, 2 * P, 3 * P
C_COS = 4 * P
C_SIN = C_COS + T
C_REV = C_SIN + T
C_ROW = C_REV + E
C_ALL = C_ROW + 1


class At:

    def __init__(self, k, i=None, period=4):
        self.k, self.i, self.period = k, i, period

    def __add__(self, n):
        return At(self.k + n, self.i, self.period)

    def count(self, per, extra):
        c = per * self.k + extra
        return c if self.i is None else self.i * (per * self.period) + c

    @property
    def number(self):
        return self.count(1, 0)

    def turn(self, ring, per=1, extra=0):
        c = per * (self.k // ring) + extra
        return c if self.i is None else self.i * (per * self.period // ring) + c


FIRST_STEP, LAST_STEP = -2, NB + 2


def in_order(step):
    made = [(kind, k) for b in range(FIRST_STEP, LAST_STEP + 1) for kind, k in step(b) if 0 <= k < NB]
    return {use: n for n, use in enumerate(made)}


T_USES = in_order(lambda b: [
    ("p2", b - 1), ("p3", b - 1), ("n1", b + 1), ("p0", b), ("h2", b - 2), ("p1", b),
    ("n2", b - 1)])
Q_USES = in_order(lambda b: [
    ("p3", b), ("pv", b), ("down", b - 3), ("s0", b - 2), ("p0", b + 1), ("p1", b + 1),
    ("s1", b - 2), ("p2", b + 1), ("s2", b - 2), ("s3", b - 2)])
LAYER_NORMS = in_order(lambda b: [(1, b - 1), (0, b + 2)])
SORT_STEPS = 3 + (E.bit_length() - 1) + 6


def uses_of_bank(uses, bank):
    return len(range(bank, len(uses), 2))


def use_of(kind, b, uses=T_USES):
    n = uses[kind, b.k]
    return n % 2, n // 2


def product_of(kind, b):
    return use_of(kind, b, Q_USES)


def block_program(nc, x, w_q, w_k, w_v, gate_w, sg_w, su_w, sd_w, rg_w, ru_w, rd_w, c, wmod, table, sel, out):
    with ExitStack() as ctx:
        def sb(name, shape, dt=F32):
            return ctx.enter_context(nc.sbuf_tensor(name, shape, dt))

        def sem(name):
            return ctx.enter_context(nc.semaphore(name))

        bank = [ctx.enter_context(nc.psum_tensor(f"bank{n}", [P, 512], F32)) for n in range(8)]
        sorted_rows = nc.dram_tensor("sorted_rows", (E * CAP + P, ROW), F32).ap()
        routed_rows = nc.dram_tensor("routed_rows", (TOKENS, D), F32).ap()

        w_gu = sb("w_gu", [P, E, 2 * F])
        x_all = sb("x_all", [P, NB, TILES, D])
        xs_all = sb("xs_all", [P, NB, TILES, ROW])
        tab = sb("tab", [P, C_ALL])
        w_v_full = sb("w_v_full", [P, D])
        w_qk = sb("w_qk", [P, 4, D])
        w_value = sb("w_value", [P, 2, D])
        w_router = sb("w_router", [P, E])
        w_sgu = sb("w_sgu", [P, 2, F])
        w_sd = sb("w_sd", [P, FC, D])
        gate_rows = sb("gate_rows", [P, NB, 2, D])
        mod_cols = sb("mod_cols", [P, 4, NB])
        ident_b = sb("ident_b", [P, P], BF16)
        upper_b = sb("upper_b", [P, P], BF16)
        mask_b = sb("mask_b", [P, P], BF16)
        ones_b = sb("ones_b", [P, P], BF16)
        onehot = sb("onehot", [P, NB, TILES + 1, E], BF16)
        pos_all = sb("pos_all", [P, NB, TILES], I32)
        blank = sb("blank", [P, ROW])
        minus_half = sb("minus_half", [P, TILES])

        HALF_DOWN = E // 2 * FC * D
        arena = sb("arena", [P, HALF_DOWN + 10 * 1024])
        w_down_flat = arena[:, 0:E * FC * D]
        w_down = w_down_flat.rearrange("p (e c n) -> p e c n", e=E, c=FC)
        w_gu_flat = w_gu[:, :, :].rearrange("p e n -> p (e n)")

        def carver(part):
            at = [0]

            def carve(*shape):
                n = 1
                for size in shape:
                    n *= size
                piece = part[:, at[0]:at[0] + n]
                at[0] += n
                names = "abc"[:len(shape)]
                return piece.rearrange(f"p ({' '.join(names)}) -> p {' '.join(names)}", **dict(zip(names, shape)))

            return carve

        carve = carver(arena[:, HALF_DOWN:])
        normed = carve(2, TILES, D)
        ht = carve(2, T)
        rope_parts = carve(4, T)
        qkt = carve(2, 2, T)
        values_of = carve(2, TILES, D)
        probs = carve(2, T)
        probs_t = carve(2, TILES, P)

        normed2 = sb("normed2", [P, TILES, D])
        ht2 = sb("ht2", [P, 2, T])

        stats = sb("stats", [P, 2, TILES, 6])
        mean_var = sb("mean_var", [P, 2, TILES, 2])
        var_eps = sb("var_eps", [P, 2, TILES])
        rstd = sb("rstd", [P, 2, TILES])
        neg_max = sb("neg_max", [P, TILES])
        row_sum = sb("row_sum", [P, 2, TILES])
        row_inv = sb("row_inv", [P, TILES])
        top_logit = sb("top_logit", [P, 2, TILES])
        tied = sb("tied", [P, TILES, E])
        first = sb("first", [P, TILES])
        top_exp = sb("top_exp", [P, 2, TILES])
        top_den = sb("top_den", [P, TILES])
        score = sb("score", [P, 2, TILES])
        ranks = sb("ranks", [P, 2, TILES + 1, E])
        own_rank = sb("own_rank", [P, TILES, E])
        rank_own = sb("rank_own", [P, TILES])
        c_cols = sb("c_cols", [P, NB])
        c_exp = sb("c_exp", [P, NB])
        c_den = sb("c_den", [P, NB])
        c_inv = sb("c_inv", [P, NB])
        c_silu = sb("c_silu", [P, NB])
        g_sign = sb("g_sign", [NB, 2 * D])
        g_abs = sb("g_abs", [NB, 2 * D])
        g_rows = sb("g_rows", [NB, 2 * D])
        n_pad = sb("n_pad", [P, E], I32)
        n_blocks = sb("n_blocks", [P, E], I32)
        PAD = E // 2
        ends = sb("ends", [P, 2, PAD + E])
        before_me = sb("before_me", [P, E])
        blocks_before = sb("blocks_before", [P, E])
        own_before = sb("own_before", [P, 1])
        expert_col = sb("expert_col", [P, 1])
        row_col = sb("row_col", [P, 1])
        expert_row = sb("expert_row", [1, P], I32)
        first_row = sb("first_row", [1, P], I32)
        used_blocks = sb("used_blocks", [1, 1], I32)
        blank_row = sb("blank_row", [1, E], I32)

        sh_tanh = sb("sh_tanh", [P, 2, T // 2])
        sh_silu = sb("sh_silu", [P, 2, T // 2])
        sh_act_t = sb("sh_act_t", [P, 2, FC, T // 2])
        sh_gated = sb("sh_gated", [P, TILES, D])
        carve = carver(xs_all[:, :, :, :].rearrange("p b j d -> p (b j d)"))
        rows_in = carve(4, ROW)
        rows_t = carve(2, P)
        r_silu = carve(2, F)
        r_act = carve(2, F)
        r_act_t = carve(2, FC, P)
        rows_out = carve(4, D)
        ids_out = sb("ids_out", [P, 4], I32)
        carve = carver(w_gu_flat[:, (E - 8) * 2 * F:])
        sel_all = carve(NB, P)
        sel_sb = sel_all[0:NB]
        wmod_sb = carve(6 * D)
        w_rep = carve(3, D)
        base_tiles = w_gu_flat[:, 0:NB * T].rearrange("p (b n) -> p b n", b=NB)

        ident = tab[:, C_ID:C_ID + P]
        cosines = tab[:, C_COS:C_SIN]
        sines = tab[:, C_SIN:C_REV]
        reversed_e = tab[:, C_REV:C_REV + E]
        row_number = tab[:, C_ROW:C_ROW + 1]
        x_tok = x.rearrange("b (j p) d -> p b j d", p=P)
        out_tok = out.rearrange("b (j p) d -> p b j d", p=P)
        routed_tok = routed_rows.rearrange("(b j p) d -> p b j d", p=P, j=TILES)

        s_table = sem("s_table")
        s_angles = sem("s_angles")
        s_router = sem("s_router")
        s_cond = sem("s_cond")
        s_sel = sem("s_sel")
        s_weights = sem("s_weights")
        s_x = [sem("s_x_first"), sem("s_x_rest")]
        s_shared_w = sem("s_shared_w")
        s_routed_w = sem("s_routed_w")
        s_down_w = [sem(f"s_down_w{n}") for n in range(E // 8)]
        blank_made = sem("blank_made")
        spare_kept = sem("spare_kept")
        blank_kept = [sem(f"blank_kept{n}") for n in range(4)]
        ids_made = sem("ids_made")
        consts_made = sem("consts_made")
        CONSTS = 6
        pool_consts = sem("pool_consts")
        c_exp_done = sem("c_exp_done")
        c_step = sem("c_step")
        mod_full = sem("mod_full")
        mod_out = sem("mod_out")
        g_step = sem("g_step")
        G_STEPS = 5
        rows_full = sem("rows_full")
        rows_out_done = sem("rows_out_done")
        w_made = sem("w_made")
        wv_ready = sem("wv_ready")
        stat_done = sem("stat_done")
        aggr_done = sem("aggr_done")
        eps_done = sem("eps_done")
        rstd_done = sem("rstd_done")
        norm1_done = sem("norm1_done")
        norm2_done = sem("norm2_done")
        t_full = [sem("t_full0"), sem("t_full1")]
        t_out = [sem("t_out0"), sem("t_out1")]
        q_full = [sem("q_full0"), sem("q_full1")]
        q_out = [sem("q_out0"), sem("q_out1")]
        rot_done = sem("rot_done")
        s_full = sem("s_full")
        max_done = sem("max_done")
        exp_done = sem("exp_done")
        y_full = sem("y_full")
        inv_done = sem("inv_done")
        x2_done = sem("x2_done")
        r_full = sem("r_full")
        r_step = sem("r_step")
        top_done = sem("top_done")
        sig_exp = sem("sig_exp")
        score_done = sem("score_done")
        onehot_done = sem("onehot_done")
        rank_step = sem("rank_step")
        sort_step = sem("sort_step")
        pos_done = sem("pos_done")
        expert_full = sem("expert_full")
        expert_done = sem("expert_done")
        blank_rows_done = sem("blank_rows_done")
        tanh_done = sem("tanh_done")
        silu_done = sem("silu_done")
        gated = sem("gated")
        base_done = sem("base_done")
        scattered = sem("scattered")
        rows_in_s = [sem(f"rows_in_s{n}") for n in range(4)]
        ids_kept = sem("ids_kept")
        c_tfull = sem("c_tfull")
        c_tout = sem("c_tout")
        c_gfull = sem("c_gfull")
        c_silu_done = sem("c_silu_done")
        c_act = sem("c_act")
        c_afull = sem("c_afull")
        c_aout = sem("c_aout")
        c_dfull = sem("c_dfull")
        c_dout = sem("c_dout")
        unsorted = [sem(f"unsorted{n}") for n in range(4)]
        final_in = [sem(f"final_in{n}") for n in range(NB)]
        final_mul = sem("final_mul")
        pool_mul = sem("pool_mul")
        pool_sum = sem("pool_sum")
        final_done = sem("final_done")
        stored = sem("stored")

        BT = bank[0:2]
        BQ = bank[2:4]
        BS = bank[4:6]
        BY = bank[6]
        BR = bank[7]
        logits = BR[:, 0:TILES * E].rearrange("p (j e) -> p j e", e=E)
        R0 = 256
        rank_ps = BR[:, R0:R0 + (TILES + 1) * E].rearrange("p (j e) -> p j e", e=E)

        def batches(step, between=lambda: None):
            for k in range(FIRST_STEP, LAST_STEP + 1):
                step(At(k))
                if k == -1:
                    between()

        def blocks(eng, step):
            part[:] = PARTS[0:2]
            for k in range(PARTS[0] - 1, PARTS[1] + 2):
                step(At(k))
            if eng is not nc.tensor:
                eng.wait_ge(expert_done, 3)
            used = eng.value_load(used_blocks[0:1, 0:1], min_val=0, max_val=BLOCKS)
            for n in range(1, len(PARTS) - 1):
                with eng.If(used > PARTS[n]):
                    part[:] = PARTS[n:n + 2]
                    for k in range(PARTS[n] - 1, PARTS[n + 1] + 2):
                        step(At(k))

        part = [0, 0]

        def in_part(b):
            return part[0] <= b.k < part[1]

        def in_range(b, n):
            return 0 <= b.k < n

        def row_starts(engine, table, b, most):
            _, rows = nc.values_load_multi_w_load_instructions(
                table[0:1, b:b + 4] if isinstance(b, int) else table[0:1, bass.ds(b, 4)],
                engines=[engine], min_val=0, max_val=most,
                skip_runtime_bounds_check_because="DVE makes them from counts of at most TOKENS rows in E experts")
            return rows

        def blank_starts(engine, g):
            return row_starts(engine, blank_row, 4 * g, E * CAP - P)

        def blank_out(eng, row, g):
            eng.dma_start(sorted_rows[bass.ds(row, P), :], blank[:, :]).then_inc(blank_kept[g % 4], 16)

        def layer_norm_turn(b, n):
            return LAYER_NORMS[n, b.k] + 1

        block = ctx.enter_context(nc.Block())

        @block.sync
        def _(sp):
            sp.dma_start(c_cols[:, :], c.rearrange("b d -> d b"), allow_slow_non_contiguous=True).then_inc(s_cond, 16)
            sp.dma_start(wmod_sb[:, :], wmod).then_inc(s_cond, 16)
            sp.dma_start(x_all[:, 0], x_tok[:, 0]).then_inc(s_x[0], 16)
            for n, w in enumerate((w_q, w_k, w_v)):
                sp.dma_start(w_rep[:, n],
                             w.rearrange("q d h -> q (d h)").unsqueeze(1).broadcast_to([HEAD_D, HEADS, D])
                             ).then_inc(s_weights, 16)
            sp.dma_start(tab[:, 0:C_COS], table[:, 0:C_COS]).then_inc(s_table, 16)
            sp.dma_start(sel_sb[:, :, :], sel).then_inc(s_sel, 16)
            sp.dma_start(tab[:, C_COS:], table[:, C_COS:]).then_inc(s_angles, 16)
            sp.dma_start(w_router[:, :], gate_w).then_inc(s_router, 16)
            for b in range(1, NB):
                sp.dma_start(x_all[:, b], x_tok[:, b]).then_inc(s_x[1], 16)
            sp.dma_start(w_sgu[:, 0], sg_w).then_inc(s_shared_w, 16)
            sp.dma_start(w_sgu[:, 1], su_w).then_inc(s_shared_w, 16)
            sp.dma_start(w_sd[:, :, :], sd_w.rearrange("(c p) n -> p c n", p=P)).then_inc(s_shared_w, 16)
            sp.wait_ge(blank_made, 2)
            sp.dma_start(sorted_rows[E * CAP:E * CAP + P, :], blank[:, :]).then_inc(spare_kept, 16)
            for e in range(0, E, 8):
                if e == E - 8:
                    sp.wait_ge(rows_full, NB // 2)
                    sp.wait_ge(w_made, 3)
                sp.dma_start(w_gu[:, e:e + 8, 0:F], rg_w[e:e + 8].rearrange("e p n -> p e n")).then_inc(s_routed_w, 16)
                sp.dma_start(w_gu[:, e:e + 8, F:2 * F], ru_w[e:e + 8].rearrange("e p n -> p e n")).then_inc(s_routed_w, 16)

            def load_down(e):
                sp.dma_start(w_down[:, e:e + 8], rd_w[e:e + 8].rearrange("e (c p) n -> p e c n", p=P)
                             ).then_inc(s_down_w[e // 8], 16)

            load_down(0)
            load_down(8)
            sp.wait_ge(rot_done, 2 * NB)
            bk, before = product_of("pv", At(NB - 1))
            sp.wait_ge(q_full[bk], before + 1)
            load_down(16)
            load_down(24)

            sp.wait_ge(blank_rows_done, 1)
            for row in blank_starts(mybir.EngineType.SP, 0):
                blank_out(sp, row, 0)

            sp.wait_ge(spare_kept, 16)
            sp.wait_ge(scattered, 16 * TILES * NB)
            sp.wait_ge(expert_done, 3)

            def load_rows(g, more_blanks=None):
                behind = blank_starts(mybir.EngineType.SP, more_blanks) if more_blanks else None
                for n, row in enumerate(row_starts(mybir.EngineType.SP, first_row, g.count(4, 0), E * CAP)):
                    if g.k >= 1:
                        sp.wait_ge(c_tfull, g.count(4, n - 3))
                        sp.wait_ge(ids_kept, g.count(4, n - 3))
                    if g.i is not None or 4 * g.k + n < BLOCKS:
                        sp.dma_start(rows_in[:, n], sorted_rows[bass.ds(row, P), :]).then_inc(rows_in_s[n], 16)
                    if behind:
                        blank_out(sp, behind[n], more_blanks)

            for g in range(E // 4):
                sp.wait_ge(blank_kept[g % 4], 4 * 16 * (g // 4 + 1))
                load_rows(At(g), g + 4 if g < 4 else None)
            with sp.Fori(0, (PARTS[1] - E) // 4) as i:
                load_rows(At(E // 4, i, 1))

            def landed(end):
                for n in range(4):
                    sp.wait_ge(unsorted[n], 16 * len(range(n, end, 4)))

            used = sp.value_load(used_blocks[0:1, 0:1], min_val=0, max_val=BLOCKS)
            for n in range(1, len(PARTS) - 1):
                with sp.If(used > PARTS[n]):
                    for g in range(PARTS[n] // 4, (PARTS[n + 1] + 3) // 4):
                        load_rows(At(g))
                    landed(PARTS[n + 1])
            landed(PARTS[1])

            for b in range(NB):
                sp.dma_start(base_tiles[:, b].rearrange("p (j d) -> p j d", j=TILES), routed_tok[:, b]
                             ).then_inc(final_in[b], 16)
            for b in range(NB):
                if b in POOL_SUMS:
                    sp.wait_ge(pool_sum, POOL_SUMS.index(b) + 1)
                else:
                    sp.wait_ge(final_done, DVE_SUMS.index(b) + 1)
                sp.dma_start(out_tok[:, b], x_all[:, b]).then_inc(stored, 16)
            sp.wait_ge(stored, 16 * NB)

        @block.gpsimd
        def _(pool):
            nc.gpsimd.memset(blank[:, :], 0.0).then_inc(blank_made, 1)
            pool.wait_ge(blank_made, 1)
            nc.gpsimd.iota(blank[:, D:ROW].bitcast(I32), [[0, 1]], base=TOKENS, channel_multiplier=1
                           ).then_inc(blank_made, 1)
            nc.gpsimd.iota(xs_all[:, :, :, D].bitcast(I32), [[T, NB], [P, TILES]], base=0, channel_multiplier=1
                           ).then_inc(ids_made, 1)
            nc.gpsimd.memset(minus_half[:, :], -0.5).then_inc(pool_consts, 1)
            pool.wait_ge(pool_consts, 1)
            pool.wait_ge(s_table, 16)
            for made, column in ((ident_b, C_ID), (upper_b, C_UP), (mask_b, C_MASK)):
                nc.gpsimd.tensor_copy(made[:, :], tab[:, column:column + P]).then_inc(consts_made, 1)

            def rstd_of(b, n):
                pool.wait_ge(aggr_done, layer_norm_turn(b, n))
                nc.gpsimd.tensor_scalar(var_eps[:, n], mean_var[:, n, :, 1], EPS, None, ALU.add).then_inc(eps_done, 1)
                pool.wait_ge(eps_done, layer_norm_turn(b, n))
                nc.gpsimd.tensor_tensor(rstd[:, n], var_eps[:, n], minus_half[:, :], ALU.pow).then_inc(rstd_done, 1)

            def value_weights(b):
                if b.k >= 2:
                    bk, before = product_of("pv", b + -2)
                    pool.wait_ge(q_full[bk], before + 1)
                pool.wait_ge(rows_out_done, b.k // 2 + 1)
                if b.k == 0:
                    pool.wait_ge(w_made, 5)
                nc.gpsimd.tensor_tensor(w_value[:, b.k % 2], w_v_full[:, :], gate_rows[:, b.k, 0], ALU.mult
                                        ).then_inc(wv_ready, 1)

            def rotate(b, m):
                for n in (2 * m, 2 * m + 1):
                    bk, before = product_of(f"p{n}", b)
                    pool.wait_ge(q_out[bk], before + 1)
                if b.k >= 2:
                    pool.wait_ge(s_full, b.count(TILES, -TILES))
                nc.gpsimd.tensor_tensor(qkt[:, b.k % 2, m], rope_parts[:, 2 * m], rope_parts[:, 2 * m + 1], ALU.add
                                        ).then_inc(rot_done, 1)

            def scatter(b, j):
                if j == 0:
                    bk, before = use_of("h2", b)
                    pool.wait_ge(t_out[bk], before + 1)
                    pool.wait_ge(pos_done, b.k + 1)
                nc.gpsimd.indirect_dma_start(
                    out=sorted_rows, out_offset=bass.IndirectOffsetOnAxis(ap=pos_all[:, b.k, j:j + 1], axis=0),
                    in_=xs_all[:, b.k, j], in_offset=None).then_inc(scattered, 16)

            def step(b):
                if in_range(b + -3, NB):
                    scatter(b + -3, 0)
                if in_range(b + 2, NB):
                    rstd_of(b + 2, 0)
                if in_range(b + -3, NB):
                    scatter(b + -3, 1)
                if in_range(b + 1, NB):
                    rotate(b + 1, 0)
                if in_range(b + -3, NB):
                    scatter(b + -3, 2)
                if in_range(b + 2, NB):
                    value_weights(b + 2)
                if in_range(b + -3, NB):
                    scatter(b + -3, 3)
                if in_range(b + 1, NB):
                    rotate(b + 1, 1)
                if in_range(b, NB):
                    rstd_of(b, 1)

            pool.wait_ge(ids_made, 1)
            batches(step)

            def block_step(b):
                if in_part(b):
                    r = b.k % 4
                    if b.k >= 4:
                        pool.wait_ge(unsorted[r], b.turn(4, 16, 0))
                    pool.wait_ge(rows_in_s[r], b.turn(4, 16, 16))
                    nc.gpsimd.tensor_copy(ids_out[:, r:r + 1], rows_in[:, r, D:ROW].bitcast(I32)).then_inc(ids_kept, 1)
                o = b + -2
                if in_part(o):
                    r = o.k % 4
                    pool.wait_ge(ids_kept, o.count(1, 1))
                    pool.wait_ge(c_dout, o.count(1, 1))
                    nc.gpsimd.indirect_dma_start(
                        out=routed_rows, out_offset=bass.IndirectOffsetOnAxis(ap=ids_out[:, r:r + 1], axis=0),
                        in_=rows_out[:, r], in_offset=None, bounds_check=TOKENS - 1, oob_is_err=False).then_inc(unsorted[r], 16)

            blocks(nc.gpsimd, block_step)

            for n, b in enumerate(POOL_SUMS):
                pool.wait_ge(final_in[b], 16)
                pool.wait_ge(base_done, NB + 1)
                rows = base_tiles[:, b].rearrange("p (j d) -> p j d", j=TILES)
                nc.gpsimd.tensor_tensor(rows, rows, gate_rows[:, b, 1:2].broadcast_to([P, TILES, D]), ALU.mult
                                        ).then_inc(pool_mul, 1)
                pool.wait_ge(pool_mul, n + 1)
                nc.gpsimd.tensor_tensor(x_all[:, b], x_all[:, b], rows, ALU.add).then_inc(pool_sum, 1)

        @block.tensor
        def _(pe):
            pe.wait_ge(s_cond, 32)
            pe.wait_ge(c_step, 3)
            for n, part in enumerate((0, 1, 3, 4)):
                nc.tensor.matmul(BR[:, n * NB:(n + 1) * NB], wmod_sb[:, part * D:(part + 1) * D], c_silu[:, :],
                                 start=True, stop=True)
            for n, part in enumerate((2, 5)):
                last = nc.tensor.matmul(BY[0:NB, n * D:(n + 1) * D], c_silu[:, :], wmod_sb[:, part * D:(part + 1) * D],
                                        start=True, stop=True)
            last.then_inc(mod_full, 1)

            def gate_rows_of(n):
                pe.wait_ge(g_step, G_STEPS)
                pe.wait_ge(s_sel, 16)
                if n >= 2:
                    pe.wait_ge(rows_out_done, n - 1)
                for m in range(2):
                    last = nc.tensor.matmul(BS[n % 2][:, m * 2 * D:(m + 1) * 2 * D], sel_sb[:, 2 * n + m], g_rows[:, :],
                                            start=True, stop=True)
                last.then_inc(rows_full, 1)

            def bank_for(kind, b):
                bk, before = use_of(kind, b)
                if before:
                    pe.wait_ge(t_out[bk], before)
                return BT[bk], t_full[bk]

            def product_bank(kind, b):
                bk, before = product_of(kind, b)
                if before:
                    pe.wait_ge(q_out[bk], before)
                return BQ[bk], q_full[bk]

            def read_out(kind, b):
                bk, before = use_of(kind, b)
                pe.wait_ge(t_out[bk], before + 1)

            def normed_t(b):
                pe.wait_ge(norm1_done, b.count(1, 1))
                to, full = bank_for("n1", b)
                for j in range(TILES):
                    last = nc.tensor.transpose(to[:, j * P:(j + 1) * P], normed[:, b.k % 2, j], ident)
                last.then_inc(full, 1)

            def project(b, n):
                if n == 0:
                    read_out("n1", b)
                to, full = product_bank(f"p{n}", b)
                nc.tensor.matmul(to[:, :], w_qk[:, n], ht[:, b.k % 2], start=True, stop=True).then_inc(full, 1)

            def project_values(b):
                pe.wait_ge(wv_ready, b.count(1, 1))
                to, full = product_bank("pv", b)
                for j in range(TILES):
                    last = nc.tensor.matmul(to[:, j * D:(j + 1) * D], ht[:, b.k % 2, j * P:(j + 1) * P],
                                            w_value[:, b.k % 2], start=True, stop=True)
                last.then_inc(full, 1)

            def scores(b, j):
                if j == 0:
                    pe.wait_ge(rot_done, b.count(2, 2))
                if b.k == 0 and j < 2:
                    pe.wait_ge(rows_out_done, NB // 2)
                else:
                    pe.wait_ge(exp_done, b.count(TILES, j - 1))
                nc.tensor.matmul(BS[j % 2][:, 0:(j + 1) * P], qkt[:, b.k % 2, 0, j * P:(j + 1) * P],
                                 qkt[:, b.k % 2, 1, 0:(j + 1) * P], start=True, stop=True)
                nc.tensor.matmul(BS[j % 2][:, j * P:(j + 1) * P], ident_b[:, :], mask_b[:, :],
                                 start=False, stop=True, skip_group_check=True).then_inc(s_full, 1)

            def probs_turned(b, j):
                pe.wait_ge(exp_done, b.count(TILES, j + 1))
                to, full = bank_for(f"p{j}", b)
                for k in range(j + 1):
                    last = nc.tensor.transpose(to[:, k * P:(k + 1) * P], probs[:, j % 2, k * P:(k + 1) * P], ident)
                last.then_inc(full, 1)

            def values(b, j):
                read_out(f"p{j}", b)
                if j == 0:
                    bk, before = product_of("pv", b)
                    pe.wait_ge(q_out[bk], before + 1)
                if j == 0 and b.k > 0:
                    pe.wait_ge(x2_done, b.count(1, 0))
                for k in range(j + 1):
                    last = nc.tensor.matmul(BY[:, j * D:(j + 1) * D], probs_t[:, j % 2, k],
                                            values_of[:, b.k % 2, k], start=(k == 0), stop=(k == j))
                last.then_inc(y_full, 1)

            def second_t(b):
                pe.wait_ge(norm2_done, b.count(1, 1))
                to, full = bank_for("n2", b)
                for j in range(TILES):
                    last = nc.tensor.transpose(to[:, j * P:(j + 1) * P], normed2[:, j], ident)
                last.then_inc(full, 1)

            def route(b):
                if b.k == 0:
                    pe.wait_ge(s_router, 16)
                read_out("n2", b)
                pe.wait_ge(rank_step, b.count(3, 0) if b.k else 1)
                for j in range(TILES):
                    last = nc.tensor.matmul(logits[:, j], ht2[:, b.k % 2, j * P:(j + 1) * P], w_router[:, :],
                                            start=True, stop=True)
                last.then_inc(r_full, 1)

            def rows_again(b):
                to, full = bank_for("h2", b)
                for j in range(TILES):
                    last = nc.tensor.transpose(to[:, j * P:(j + 1) * P], ht2[:, b.k % 2, j * P:(j + 1) * P], ident)
                last.then_inc(full, 1)

            def rank(b):
                pe.wait_ge(onehot_done, b.count(1, 1))
                nc.tensor.matmul(rank_ps, upper_b[:, :], onehot[:, b.k], start=True, stop=True)
                for j in range(TILES):
                    last = nc.tensor.matmul(rank_ps[:, j + 1:], ones_b[:, :],
                                            onehot[:, b.k, j:j + 1].broadcast_to([P, TILES - j, E]),
                                            start=False, stop=True, skip_group_check=True)
                last.then_inc(r_full, 1)

            def shared_up(b, n):
                half, ch = n // FC, n % FC
                if b.k == 0 and n == 0:
                    pe.wait_ge(s_shared_w, 48)
                to, full = product_bank(f"s{n}", b)
                for gu in range(2):
                    last = nc.tensor.matmul(to[:, gu * T // 2:(gu + 1) * T // 2], w_sgu[:, gu, ch * P:(ch + 1) * P],
                                            ht2[:, b.k % 2, half * T // 2:(half + 1) * T // 2], start=True, stop=True)
                last.then_inc(full, 1)

            def shared_down(b):
                for n in range(2 * FC):
                    bk, before = product_of(f"s{n}", b)
                    pe.wait_ge(q_out[bk], before + 1)
                to, full = product_bank("down", b)
                for j in range(TILES):
                    for ch in range(FC):
                        last = nc.tensor.matmul(to[:, j * D:(j + 1) * D],
                                                sh_act_t[:, j // 2, ch, (j % 2) * P:(j % 2 + 1) * P], w_sd[:, ch],
                                                start=(ch == 0), stop=(ch == FC - 1))
                last.then_inc(full, 1)

            def table_rows():
                pe.wait_ge(sort_step, SORT_STEPS)
                nc.tensor.matmul(BR[0:1, 0:P], expert_col[:, :], ident, start=True, stop=True)
                nc.tensor.matmul(BR[0:1, P:2 * P], row_col[:, :], ident, start=True, stop=True).then_inc(expert_full, 1)

            def step(b):
                if in_range(b + -1, NB):
                    values(b + -1, 1)
                    probs_turned(b + -1, 2)
                if in_range(b + -2, NB):
                    route(b + -2)
                if in_range(b + -1, NB):
                    probs_turned(b + -1, 3)
                if in_range(b, NB):
                    project(b, 3)
                if in_range(b + -1, NB):
                    values(b + -1, 2)
                    values(b + -1, 3)
                if in_range(b, NB):
                    project_values(b)
                if in_range(b + -3, NB):
                    shared_down(b + -3)
                if in_range(b + 1, NB):
                    normed_t(b + 1)
                if in_range(b + -2, NB):
                    shared_up(b + -2, 0)
                if in_range(b, NB):
                    scores(b, 0)
                if in_range(b + -2, NB):
                    rank(b + -2)
                if in_range(b, NB):
                    scores(b, 1)
                if in_range(b + 1, NB):
                    project(b + 1, 0)
                    project(b + 1, 1)
                if in_range(b, NB):
                    scores(b, 2)
                    probs_turned(b, 0)
                if in_range(b + -2, NB):
                    rows_again(b + -2)
                    shared_up(b + -2, 1)
                if in_range(b, NB):
                    scores(b, 3)
                    probs_turned(b, 1)
                if in_range(b + 1, NB):
                    project(b + 1, 2)
                if in_range(b, NB):
                    values(b, 0)
                if in_range(b + -2, NB):
                    shared_up(b + -2, 2)
                if in_range(b + -1, NB):
                    second_t(b + -1)
                if in_range(b + -2, NB):
                    shared_up(b + -2, 3)
                if (b + -2).k == NB - 1:
                    table_rows()

            def other_gates():
                for n in range(1, NB // 2):
                    gate_rows_of(n)
                pe.wait_ge(mod_out, 2)
                pe.wait_ge(consts_made, CONSTS)

            gate_rows_of(0)
            pe.wait_ge(s_table, 16)
            pe.wait_ge(w_made, 5)
            batches(step, other_gates)

            for n in range(2):
                pe.wait_ge(q_out[n], uses_of_bank(Q_USES, n))
            pe.wait_ge(s_routed_w, 16 * 2 * E // 8)
            pe.wait_ge(expert_done, 3)

            def rows_turned(b):
                pe.wait_ge(rows_in_s[b.k % 4], b.turn(4, 16, 16))
                if b.k >= 2:
                    pe.wait_ge(c_tout, b.count(1, -1))
                nc.tensor.transpose(bank[b.k % 2][:, 0:P], rows_in[:, b.k % 4, 0:D], ident).then_inc(c_tfull, 1)

            at = {}

            def experts_of(k):
                n = min(BLOCKS_PER_LOAD, BLOCKS - k)
                _, values = nc.values_load_multi_w_load_instructions(
                    expert_row[0:1, k:k + n], engines=[mybir.EngineType.PE], min_val=0, max_val=(E - 1) * FC * D,
                    skip_runtime_bounds_check_because="DVE counts at most E experts and takes the minimum with E - 1")
                for m, value in enumerate(values):
                    at[k + m] = value

            def expert_up(b):
                pe.wait_ge(c_tout, b.count(1, 1))
                if b.k >= 2:
                    pe.wait_ge(c_act, b.count(1, -1))
                nc.tensor.matmul(bank[2 + b.k % 2][:, :], rows_t[:, b.k % 2],
                                 w_gu_flat[:, bass.ds(at[b.k] * (2 * F // (FC * D)), 2 * F)], start=True, stop=True).then_inc(c_gfull, 1)

            def act_turned(b):
                pe.wait_ge(c_act, b.count(1, 1))
                if b.k >= 2:
                    pe.wait_ge(c_aout, b.count(1, -1))
                for ch in range(FC):
                    last = nc.tensor.transpose(bank[4 + b.k % 2][:, ch * P:(ch + 1) * P],
                                               r_act[:, b.k % 2, ch * P:(ch + 1) * P], ident)
                last.then_inc(c_afull, 1)

            def expert_down(b):
                pe.wait_ge(c_aout, b.count(1, 1))
                if b.k >= 2:
                    pe.wait_ge(c_dout, b.count(1, -1))
                for ch in range(FC):
                    last = nc.tensor.matmul(bank[6 + b.k % 2][:, 0:D], r_act_t[:, b.k % 2, ch],
                                            w_down_flat[:, bass.ds(at[b.k] + ch * D, D)],
                                            start=(ch == 0), stop=(ch == FC - 1))
                last.then_inc(c_dfull, 1)

            def block_step(b):
                if in_part(b + 1):
                    rows_turned(b + 1)
                if in_part(b):
                    if b.k % BLOCKS_PER_LOAD == 0:
                        experts_of(b.k)
                        if b.k < E:
                            pe.wait_ge(s_down_w[b.k // 8], 16)
                    expert_up(b)
                if in_part(b + -2):
                    expert_down(b + -2)
                if in_part(b + -1):
                    act_turned(b + -1)

            blocks(nc.tensor, block_step)

        @block.scalar
        def _(act):
            act.wait_ge(s_cond, 32)
            nc.scalar.activation(c_exp[:, :], c_cols[:, :], ACT.Exp, scale=-1.0).then_inc(c_exp_done, 1)

            def gates_out(n):
                act.wait_ge(rows_full, n + 1)
                nc.scalar.copy(gate_rows[:, 2 * n:2 * n + 2].rearrange("p b g d -> p (b g d)"), BS[n % 2][:, :]
                               ).then_inc(rows_out_done, 1)

            def full(kind, b):
                bk, before = use_of(kind, b)
                act.wait_ge(t_full[bk], before + 1)
                return BT[bk], t_out[bk]

            def modulated_out(b, kind, dest, n):
                frm, done = full(kind, b)
                nc.scalar.activation(dest[:, b.k % 2], frm[:, :], ACT.Identity,
                                     bias=mod_cols[:, n, b.k:b.k + 1],
                                     scale=mod_cols[:, n + 1, b.k:b.k + 1]).then_inc(done, 1)

            def exponentials(b, j):
                act.wait_ge(max_done, b.count(TILES, j + 1))
                kind, of = (f"p{j - 2}", b) if j >= 2 else (f"p{j + 2}", b + -1)
                if of.k >= 0:
                    bk, before = use_of(kind, of)
                    act.wait_ge(t_full[bk], before + 1)
                nc.scalar.activation(probs[:, j % 2, 0:(j + 1) * P], BS[j % 2][:, 0:(j + 1) * P], ACT.Exp,
                                     bias=neg_max[:, j:j + 1], scale=1.0,
                                     accum_out=row_sum[:, b.k % 2, j:j + 1]).then_inc(exp_done, 1)

            def values_out(b):
                bk, before = product_of("pv", b)
                act.wait_ge(q_full[bk], before + 1)
                if b.k >= 2:
                    act.wait_ge(y_full, b.count(TILES, -TILES))
                nc.scalar.copy(values_of[:, b.k % 2].rearrange("p j d -> p (j d)"), BQ[bk][:, :]
                               ).then_inc(q_out[bk], 1)

            def probs_out(b, j):
                frm, done = full(f"p{j}", b)
                if b.count(TILES, j - 1) > 0:
                    act.wait_ge(y_full, b.count(TILES, j - 1))
                nc.scalar.copy(probs_t[:, j % 2, 0:j + 1], frm[:, 0:(j + 1) * P].rearrange("p (k t) -> p k t", t=P)
                               ).then_inc(done, 1)

            def second_out(b):
                if b.k >= 2:
                    bk, before = product_of("s3", b + -2)
                    act.wait_ge(q_full[bk], before + 1)
                    act.wait_ge(r_full, b.count(2, -3))
                    bk, before = use_of("h2", b + -2)
                    act.wait_ge(t_full[bk], before + 1)
                modulated_out(b, "n2", ht2, 2)

            def first_out(b):
                if b.k >= 2:
                    for kind in ("p3", "pv"):
                        bk, before = product_of(kind, b + -2)
                        act.wait_ge(q_full[bk], before + 1)
                modulated_out(b, "n1", ht, 0)

            def sigmoid_exp(b):
                act.wait_ge(top_done, b.count(1, 1))
                nc.scalar.activation(top_exp[:, b.k % 2], top_logit[:, b.k % 2], ACT.Exp, scale=-1.0).then_inc(sig_exp, 1)

            def scaled_out(b):
                frm, done = full("h2", b)
                act.wait_ge(score_done, b.count(1, 1))
                for j in range(TILES):
                    last = nc.scalar.activation(xs_all[:, b.k, j, 0:D], frm[:, j * P:(j + 1) * P], ACT.Copy,
                                                scale=score[:, b.k % 2, j:j + 1])
                last.then_inc(done, 1)

            def shared_tanh(b, n):
                bk, before = product_of(f"s{n}", b)
                act.wait_ge(q_full[bk], before + 1)
                if b.k > 0 or n >= 2:
                    of, out_before = product_of(f"s{(n + 2) % 4}", b if n >= 2 else b + -1)
                    act.wait_ge(q_out[of], out_before + 1)
                nc.scalar.activation(sh_tanh[:, n % 2], BQ[bk][:, 0:T // 2], ACT.Tanh, scale=0.5).then_inc(tanh_done, 1)

            def step(b):
                if in_range(b + -3, NB):
                    scaled_out(b + -3)
                if in_range(b + -1, NB):
                    exponentials(b + -1, 2)
                    probs_out(b + -1, 1)
                if in_range(b + -3, NB):
                    shared_tanh(b + -3, 2)
                if in_range(b + -2, NB):
                    second_out(b + -2)
                if in_range(b + -1, NB):
                    exponentials(b + -1, 3)
                if in_range(b + -3, NB):
                    shared_tanh(b + -3, 3)
                if in_range(b + -1, NB):
                    probs_out(b + -1, 2)
                    probs_out(b + -1, 3)
                if in_range(b, NB):
                    values_out(b)
                if in_range(b + 1, NB):
                    first_out(b + 1)
                if in_range(b + -2, NB):
                    shared_tanh(b + -2, 0)
                if in_range(b, NB):
                    exponentials(b, 0)
                if in_range(b + -2, NB):
                    sigmoid_exp(b + -2)
                if in_range(b, NB):
                    exponentials(b, 1)
                    probs_out(b, 0)
                if in_range(b + -2, NB):
                    shared_tanh(b + -2, 1)

            def other_gates():
                for n in range(1, NB // 2):
                    gates_out(n)

            gates_out(0)
            act.wait_ge(mod_out, 2)
            batches(step, other_gates)

            act.wait_ge(blank_rows_done, 1)
            for g in range(1, 4):
                for row in blank_starts(mybir.EngineType.Activation, g):
                    blank_out(nc.scalar, row, g)

            def block_step(b):
                n = b + 1
                if in_part(n):
                    act.wait_ge(c_tfull, n.count(1, 1))
                    if n.k >= 2:
                        act.wait_ge(c_gfull, n.count(1, -1))
                    nc.scalar.copy(rows_t[:, n.k % 2], bank[n.k % 2][:, 0:P]).then_inc(c_tout, 1)
                if in_part(b):
                    act.wait_ge(c_gfull, b.count(1, 1))
                    if b.k >= 2:
                        act.wait_ge(c_act, b.count(1, -1))
                    nc.scalar.activation(r_silu[:, b.k % 2], bank[2 + b.k % 2][:, 0:F], ACT.Silu).then_inc(c_silu_done, 1)
                o = b + -2
                if in_part(o):
                    act.wait_ge(c_dfull, o.count(1, 1))
                    if o.k >= 4:
                        act.wait_ge(unsorted[o.k % 4], o.turn(4, 16, 0))
                    nc.scalar.copy(rows_out[:, o.k % 4], bank[6 + o.k % 2][:, 0:D]).then_inc(c_dout, 1)

            blocks(nc.scalar, block_step)

        @block.vector
        def _(dve):
            V = nc.vector

            def statistics(b, n, early=False):
                if n == 0 and b.k == 0:
                    if not early:
                        return
                    dve.wait_ge(s_x[0], 16)
                if n == 0 and b.k == 1:
                    dve.wait_ge(s_x[1], 16 * (NB - 1))
                if n == 1:
                    dve.wait_ge(x2_done, b.count(1, 1))
                for j in range(TILES):
                    last = V.bn_stats(stats[:, n, j], x_all[:, b.k, j])
                last.then_inc(stat_done, 1)
                dve.wait_ge(stat_done, layer_norm_turn(b, n))
                for j in range(TILES):
                    last = V.bn_aggr(mean_var[:, n, j], stats[:, n, j])
                last.then_inc(aggr_done, 1)

            V.memset(ones_b[:, :], 1.0).then_inc(consts_made, 1)
            V.memset(onehot[:, :, TILES], 0.0).then_inc(consts_made, 1)
            V.memset(ends[:, :, 0:PAD], 0.0).then_inc(consts_made, 1)
            V.memset(ranks[:, 1, TILES], float(E * CAP)).then_inc(rank_step, 1)
            V.memset(own_rank[:, :, :], 0.0).then_inc(rank_step, 1)
            V.memset(sh_gated[:, :, :], 0.0).then_inc(base_done, 1)
            dve.wait_ge(c_exp_done, 1)
            V.tensor_scalar(c_den[:, :], c_exp[:, :], 1.0, None, ALU.add).then_inc(c_step, 1)
            dve.wait_ge(c_step, 1)
            V.reciprocal(c_inv[:, :], c_den[:, :]).then_inc(c_step, 1)
            dve.wait_ge(c_step, 2)
            V.tensor_tensor(c_silu[:, :], c_cols[:, :], c_inv[:, :], ALU.mult).then_inc(c_step, 1)
            statistics(At(0), 0, early=True)
            dve.wait_ge(mod_full, 1)
            cols = BR[:, 0:4 * NB].rearrange("p (a two b) -> p a two b", two=2, b=NB)
            kept = mod_cols[:, :, :].rearrange("p (a two) b -> p a two b", two=2)
            V.tensor_copy(kept[:, :, 0], cols[:, :, 0]).then_inc(mod_out, 1)
            V.tensor_scalar(kept[:, :, 1], cols[:, :, 1], 1.0, None, ALU.add).then_inc(mod_out, 1)
            g = BY[0:NB, 0:2 * D]
            V.tensor_scalar(g_sign[:, :], g, 0.0, 2.0, ALU.is_ge, ALU.mult).then_inc(g_step, 1)
            V.tensor_copy(g_abs[:, :], g).then_inc(g_step, 1)
            dve.wait_ge(g_step, 2)
            V.scalar_tensor_tensor(out=g_rows[:, :], in0=g_abs[:, :], scalar=-1.0, in1=g_abs[:, :],
                                   op0=ALU.mult, op1=ALU.max).then_inc(g_step, 1)
            dve.wait_ge(g_step, 3)
            V.tensor_scalar(g_abs[:, :], g_rows[:, :], FLOOR, None, ALU.max).then_inc(g_step, 1)
            dve.wait_ge(g_step, 4)
            V.scalar_tensor_tensor(out=g_rows[:, :], in0=g_sign[:, :], scalar=1.0, in1=g_abs[:, :],
                                   op0=ALU.subtract, op1=ALU.mult).then_inc(g_step, 1)
            dve.wait_ge(s_weights, 16 * 3)
            dve.wait_ge(s_table, 16)
            head = tab[:, C_HEAD:C_HEAD + D]
            V.scalar_tensor_tensor(out=w_qk[:, 0], in0=w_rep[:, 0], scalar=GAMMA, in1=head,
                                   op0=ALU.mult, op1=ALU.mult).then_inc(w_made, 1)
            V.tensor_tensor(w_qk[:, 2], w_rep[:, 1], head, ALU.mult).then_inc(w_made, 1)
            V.tensor_tensor(w_v_full[:, :], w_rep[:, 2], head, ALU.mult).then_inc(w_made, 1)
            dve.wait_ge(w_made, 3)
            of_pairs = w_qk[:, :, :].rearrange("p (a two) (i h) -> p a two i h", two=2, h=2)
            for h in range(2):
                V.tensor_copy(of_pairs[:, :, 1, :, h], of_pairs[:, :, 0, :, 1 - h]).then_inc(w_made, 1)

            def normalise(b, n):
                dve.wait_ge(rstd_done, layer_norm_turn(b, n))
                if n == 0 and b.k >= 2:
                    bk, before = use_of("n1", b + -2)
                    dve.wait_ge(t_full[bk], before + 1)
                if n == 1 and b.k >= 1:
                    bk, before = use_of("n2", b + -1)
                    dve.wait_ge(t_full[bk], before + 1)
                for j in range(TILES):
                    dest = normed2[:, j] if n else normed[:, b.k % 2, j]
                    last = V.tensor_scalar(dest, x_all[:, b.k, j], mean_var[:, n, j, 0:1], rstd[:, n, j:j + 1],
                                           ALU.subtract, ALU.mult)
                last.then_inc(norm2_done if n else norm1_done, 1)

            def rope_part(b, n):
                if b.k == 0 and n == 0:
                    dve.wait_ge(s_angles, 16)
                bk, before = product_of(f"p{n}", b)
                dve.wait_ge(q_full[bk], before + 1)
                if b.k > 0:
                    dve.wait_ge(rot_done, b.count(2, n // 2 - 1))
                V.tensor_tensor(rope_parts[:, n], BQ[bk][:, :], sines if n % 2 else cosines, ALU.mult
                                ).then_inc(q_out[bk], 1)

            def row_max(b, j):
                dve.wait_ge(s_full, b.count(TILES, j + 1))
                if b.k > 0:
                    dve.wait_ge(exp_done, b.count(TILES, j + 1 - TILES))
                V.tensor_reduce(neg_max[:, j:j + 1], BS[j % 2][:, 0:(j + 1) * P], AX.X, ALU.max, negate=True
                                ).then_inc(max_done, 1)

            def attention_out(b):
                dve.wait_ge(y_full, b.count(TILES, TILES))
                V.reciprocal(row_inv[:, :], row_sum[:, b.k % 2]).then_inc(inv_done, 1)
                dve.wait_ge(inv_done, b.count(1, 1))
                for j in range(TILES):
                    last = V.scalar_tensor_tensor(out=x_all[:, b.k, j], in0=BY[:, j * D:(j + 1) * D],
                                                  scalar=row_inv[:, j:j + 1], in1=x_all[:, b.k, j],
                                                  op0=ALU.mult, op1=ALU.add)
                last.then_inc(x2_done, 1)

            def choose(b):
                dve.wait_ge(r_full, b.count(2, 1))
                V.tensor_reduce(top_logit[:, b.k % 2], logits, AX.X, ALU.max).then_inc(top_done, 1)
                dve.wait_ge(top_done, b.count(1, 1))
                V.tensor_tensor(tied[:, :, :], logits, top_logit[:, b.k % 2].unsqueeze(2).broadcast_to([P, TILES, E]),
                                ALU.is_equal).then_inc(r_step, 1)
                dve.wait_ge(r_step, b.count(3, 1))
                V.tensor_tensor(tied[:, :, :], tied[:, :, :], reversed_e.unsqueeze(1).broadcast_to([P, TILES, E]),
                                ALU.mult).then_inc(r_step, 1)
                dve.wait_ge(r_step, b.count(3, 2))
                V.tensor_reduce(first[:, :], tied[:, :, :], AX.X, ALU.max).then_inc(r_step, 1)
                dve.wait_ge(r_step, b.count(3, 3))
                V.tensor_tensor(onehot[:, b.k, 0:TILES], first[:, :].unsqueeze(2).broadcast_to([P, TILES, E]),
                                reversed_e.unsqueeze(1).broadcast_to([P, TILES, E]), ALU.is_equal
                                ).then_inc(onehot_done, 1)

            def score_of(b):
                dve.wait_ge(sig_exp, b.count(1, 1))
                V.tensor_scalar(top_den[:, :], top_exp[:, b.k % 2], 1.0, None, ALU.add).then_inc(g_step, 1)
                dve.wait_ge(g_step, b.count(1, G_STEPS + 1))
                V.reciprocal(score[:, b.k % 2], top_den[:, :]).then_inc(score_done, 1)

            def ranks_out(b):
                dve.wait_ge(r_full, b.count(2, 2))
                V.tensor_tensor(ranks[:, b.k % 2], rank_ps,
                                ranks[:, (b.k + 1) % 2, TILES:TILES + 1].broadcast_to([P, TILES + 1, E]), ALU.add
                                ).then_inc(rank_step, 1)
                dve.wait_ge(rank_step, b.count(3, 3))
                V.tensor_tensor(own_rank[:, :, :], ranks[:, b.k % 2, 0:TILES], onehot[:, b.k, 0:TILES], ALU.mult
                                ).then_inc(rank_step, 1)
                dve.wait_ge(rank_step, b.count(3, 4))
                V.tensor_reduce(rank_own[:, :], own_rank[:, :, :], AX.X, ALU.add).then_inc(rank_step, 1)
                dve.wait_ge(rank_step, b.count(3, 5))
                V.scalar_tensor_tensor(out=pos_all[:, b.k], in0=first[:, :], scalar=-float(CAP), in1=rank_own[:, :],
                                       op0=ALU.mult, op1=ALU.add).then_inc(pos_done, 1)

            def shared_act(b, n):
                bk, _ = product_of(f"s{n}", b)
                dve.wait_ge(tanh_done, b.count(2 * FC, n + 1))
                V.scalar_tensor_tensor(out=sh_silu[:, n % 2], in0=sh_tanh[:, n % 2], scalar=1.0, in1=BQ[bk][:, 0:T // 2],
                                       op0=ALU.add, op1=ALU.mult).then_inc(silu_done, 1)
                dve.wait_ge(silu_done, b.count(2 * FC, n + 1))
                if b.k > 0:
                    of, before = product_of("down", b + -1)
                    dve.wait_ge(q_full[of], before + 1)
                V.scalar_tensor_tensor(out=sh_act_t[:, n // FC, n % FC], in0=sh_silu[:, n % 2], scalar=0.5,
                                       in1=BQ[bk][:, T // 2:T], op0=ALU.mult, op1=ALU.mult).then_inc(q_out[bk], 1)

            def shared_out(b):
                bk, before = product_of("down", b)
                dve.wait_ge(q_full[bk], before + 1)
                dve.wait_ge(base_done, b.count(1, 1))
                V.tensor_tensor(sh_gated[:, :, :], BQ[bk][:, :].rearrange("p (j d) -> p j d", j=TILES),
                                gate_rows[:, b.k, 1:2].broadcast_to([P, TILES, D]), ALU.mult).then_inc(q_out[bk], 1)
                dve.wait_ge(q_out[bk], before + 1)
                V.tensor_tensor(x_all[:, b.k], x_all[:, b.k], sh_gated[:, :, :], ALU.add).then_inc(base_done, 1)

            def step(b):
                if in_range(b, NB):
                    rope_part(b, 0)
                if in_range(b + -2, NB):
                    normalise(b + -2, 1)
                if in_range(b + -1, NB):
                    row_max(b + -1, 2)
                if in_range(b, NB):
                    rope_part(b, 1)
                if in_range(b + -3, NB):
                    score_of(b + -3)
                    shared_act(b + -3, 1)
                if in_range(b + -1, NB):
                    row_max(b + -1, 3)
                if in_range(b, NB):
                    rope_part(b, 2)
                if in_range(b + -3, NB):
                    ranks_out(b + -3)
                if (b + -3).k == NB - 1:
                    sort()
                if in_range(b + 1, NB):
                    normalise(b + 1, 0)
                if in_range(b + -3, NB):
                    shared_act(b + -3, 2)
                    shared_act(b + -3, 3)
                if (b + -3).k == NB - 1:
                    tables_out()
                if in_range(b + -2, NB):
                    choose(b + -2)
                if in_range(b, NB):
                    rope_part(b, 3)
                if in_range(b + -1, NB):
                    attention_out(b + -1)
                    statistics(b + -1, 1)
                if in_range(b + -3, NB):
                    shared_out(b + -3)
                if in_range(b, NB):
                    row_max(b, 0)
                if in_range(b + -2, NB):
                    shared_act(b + -2, 0)
                if in_range(b, NB):
                    row_max(b, 1)
                if in_range(b + 2, NB):
                    statistics(b + 2, 0)

            steps = [0]

            def chained(ins):
                steps[0] += 1
                ins.then_inc(sort_step, 1)
                dve.wait_ge(sort_step, steps[0])

            def sort():
                counts = ranks[:, (NB - 1) % 2, TILES]
                V.scalar_tensor_tensor(out=blank_row[:, :], in0=reversed_e[0:1], scalar=-float(CAP), in1=counts[0:1],
                                       op0=ALU.mult, op1=ALU.add).then_inc(blank_rows_done, 1)
                chained(V.tensor_scalar(n_pad[:, :], counts, float(P - 1), None, ALU.add))
                chained(V.tensor_scalar(n_blocks[:, :], n_pad[:, :], P.bit_length() - 1, None, ALU.arith_shift_right))
                chained(V.tensor_scalar(ends[:, 0, PAD:], n_blocks[:, :], float(E * CAP // P), 1.0,
                                        ALU.subtract, ALU.max))
                shift, cur = 1, 0
                while shift < E:
                    chained(V.tensor_tensor(ends[:, 1 - cur, PAD:], ends[:, cur, PAD:],
                                            ends[:, cur, PAD - shift:PAD + E - shift], ALU.add))
                    shift, cur = 2 * shift, 1 - cur
                V.tensor_copy(used_blocks[:, :], ends[0:1, cur, PAD + E - 1:PAD + E]).then_inc(expert_done, 1)
                chained(V.tensor_scalar(before_me[:, :], ends[:, cur, PAD:], row_number, None, ALU.is_le))
                chained(V.tensor_reduce(expert_col[:, :], before_me[:, :], AX.X, ALU.add))
                chained(V.tensor_tensor(blocks_before[:, :], before_me[:, :], ends[:, cur, PAD:], ALU.mult))
                chained(V.tensor_reduce(own_before[:, :], blocks_before[:, :], AX.X, ALU.max))
                chained(V.scalar_tensor_tensor(out=row_col[:, :], in0=expert_col[:, :], scalar=float(CAP // P),
                                               in1=row_number, op0=ALU.mult, op1=ALU.add))
                chained(V.tensor_scalar(row_col[:, :], row_col[:, :], own_before[:, :], float(P), ALU.subtract, ALU.mult))
                assert steps[0] == SORT_STEPS

            def tables_out():
                dve.wait_ge(expert_full, 1)
                V.tensor_scalar(expert_row[:, :], BR[0:1, 0:P], float(E - 1), float(FC * D), ALU.min, ALU.mult
                                ).then_inc(expert_done, 1)
                V.tensor_scalar(first_row[:, :], BR[0:1, P:2 * P], float(E * CAP), None, ALU.min
                                ).then_inc(expert_done, 1)

            batches(step)

            def block_step(b):
                if in_part(b):
                    dve.wait_ge(c_silu_done, b.count(1, 1))
                    if b.k >= 2:
                        dve.wait_ge(c_afull, b.count(1, -1))
                    V.tensor_tensor(r_act[:, b.k % 2], r_silu[:, b.k % 2], bank[2 + b.k % 2][:, F:2 * F], ALU.mult
                                    ).then_inc(c_act, 1)
                o = b + -1
                if in_part(o):
                    dve.wait_ge(c_afull, o.count(1, 1))
                    if o.k >= 2:
                        dve.wait_ge(c_dfull, o.count(1, -1))
                    V.tensor_copy(r_act_t[:, o.k % 2], bank[4 + o.k % 2][:, 0:F].rearrange("p (c t) -> p c t", c=FC)
                                  ).then_inc(c_aout, 1)

            blocks(V, block_step)

            def gate_routed(b):
                dve.wait_ge(final_in[b], 16)
                rows = base_tiles[:, b].rearrange("p (j d) -> p j d", j=TILES)
                V.tensor_tensor(rows, rows, gate_rows[:, b, 1:2].broadcast_to([P, TILES, D]), ALU.mult
                                ).then_inc(final_mul, 1)

            gate_routed(DVE_SUMS[0])
            for n, b in enumerate(DVE_SUMS):
                if n + 1 < len(DVE_SUMS):
                    gate_routed(DVE_SUMS[n + 1])
                dve.wait_ge(final_mul, n + 1)
                V.tensor_tensor(x_all[:, b], x_all[:, b], base_tiles[:, b].rearrange("p (j d) -> p j d", j=TILES), ALU.add
                                ).then_inc(final_done, 1)


_INS = ["L0_attn_x", "L0_attn_w_q", "L0_attn_w_k", "L0_attn_w_v", "L0_ffn_gate_w", "L0_ffn_shared_gate_w",
        "L0_ffn_shared_up_w", "L0_ffn_shared_down_w", "L0_ffn_routed_gate_w", "L0_ffn_routed_up_w",
        "L0_ffn_routed_down_w", "L0_c", "L0_wmod"]


def constants():
    import numpy as np

    n = np.arange(P)
    table = np.zeros((P, C_ALL), np.float32)
    table[:, C_ID:C_ID + P] = np.eye(P)
    table[:, C_UP:C_UP + P] = n[:, None] < n[None, :]
    table[:, C_MASK:C_MASK + P] = np.where(n[None, :] > n[:, None], np.float32(-3e38), np.float32(0))
    table[:, C_HEAD:C_HEAD + D] = n[:, None] % HEADS == n[None, :] % HEADS
    half = D // 2
    inv_freq = (np.float32(1.0) / np.float32(10000.0) ** (np.arange(half, dtype=np.float32) / np.float32(half)))
    angle = np.arange(T, dtype=np.float32)[:, None] * inv_freq.astype(np.float32)[None, :]
    sin = np.sin(angle).T
    table[:, C_COS:C_SIN] = np.repeat(np.cos(angle).T, 2, axis=0)
    table[:, C_SIN:C_REV] = np.stack([-sin, sin], axis=1).reshape(D, T)
    table[:, C_REV:C_REV + E] = E - np.arange(E)
    table[:, C_ROW] = n
    sel = np.zeros((NB, NB, P), np.float32)
    for b in range(NB):
        sel[b, b] = 1.0
    return table, sel


def kernel(**inputs):
    import numpy as _np
    import concourse.bacc as _bacc
    from concourse import mybir as _mybir
    from concourse.bass_utils import run_bass_kernel_spmd as _run

    nc = _bacc.Bacc("TRN2", target_bir_lowering=False, num_devices=1)
    table, sel = constants()
    arrays, args = {}, []
    for name, a in [(n, _np.ascontiguousarray(inputs[n])) for n in _INS] + [("table", table), ("sel", sel)]:
        arrays[f"in_{name}"] = a
        args.append(nc.dram_tensor(f"in_{name}", a.shape, _mybir.dt.from_np(a.dtype), kind="ExternalInput").ap())
    args.append(nc.dram_tensor("out_0", (NB, T, D), F32, kind="ExternalOutput").ap())
    block_program(nc, *args)
    r = _run(nc, [arrays], core_ids=[0])
    return r.results[0]["out_0"]
```
